# Optimizing a Trainium2 kernel written in Bass

```python
import numpy as np
import jax
import jax.numpy as jnp

def _softmax(x, axis=-1):
    return jax.nn.softmax(x, axis=axis)

def _gelu(x):
    return jax.nn.gelu(x, approximate=True)

def _silu(x):
    return jax.nn.silu(x)

def _sigmoid(x):
    return jax.nn.sigmoid(x)

def _layernorm(x, axis=-1, eps=1e-05):
    m = jnp.mean(x, axis=axis, keepdims=True)
    v = jnp.var(x, axis=axis, keepdims=True)
    return (x - m) / jnp.sqrt(v + eps)

def _scatter_add(tgt, idx, src, axis=0):
    return tgt.at[idx].add(src)

def _segment_sum(src, seg, n):
    return jax.ops.segment_sum(src, seg, n)
kernel_name = 'mk_perceiver_d1_seqx_r2_46bd22'

def setup_inputs(seed: int=0):
    np.random.seed(seed)
    _w = jnp.asarray

    def _rec_inputs():
        import jax
        import jax.numpy as jnp
        _rk = jax.random.key(seed)
        x = -0.000125 + 0.9999 * jax.random.normal(jax.random.fold_in(_rk, 1), (16, 64, 2048), jnp.float32)
        _lenS = 64 - jax.random.randint(jax.random.fold_in(_rk, 7), (16,), 0, max(1, 64 // 4) + 1, jnp.int32)
        _lenS2 = 1601 - jax.random.randint(jax.random.fold_in(_rk, 8), (16,), 0, max(1, 1601 // 4) + 1, jnp.int32)
        _ctx_4096P = jax.random.normal(jax.random.fold_in(_rk, 11), (16, 16, 2048), jnp.float32)
        _ctx_4096c = jax.random.dirichlet(jax.random.fold_in(_rk, 511), 0.3 * jnp.ones((16,), jnp.float32), (16, 1601))
        _ctx_4096t = jnp.einsum('bsk,bkd->bsd', _ctx_4096c, _ctx_4096P)
        _ctx_4096t = _ctx_4096t * jax.lax.rsqrt(jnp.mean(jnp.square(_ctx_4096t)) + 1e-12) * 0.953939
        ctx_4096 = -1.52775e-05 + 0.999936 * (_ctx_4096t + 0.3 * jax.random.normal(jax.random.fold_in(_rk, 611), (16, 1601, 2048), jnp.float32))
        return (x, ctx_4096)
    x, ctx_4096 = _rec_inputs()

    def _L0_xattn_setup():
        import jax, jax.numpy as jnp
        import numpy as np
        import math
        EPS = 1e-05
        LAMBDA = 0.6

        def _crucial_k(C):
            f = math.floor(LAMBDA * C)
            return f + f % 2

        def _conv1d(y, w):
            return jax.lax.conv_general_dilated(y, w, window_strides=(1,), padding=((3, 3),), dimension_numbers=('NCH', 'OIH', 'NCH'))

        def _norm_active(z, gamma, beta):
            mu = jnp.mean(z, axis=(0, 2), keepdims=True)
            var = jnp.mean((z - mu) ** 2, axis=(0, 2), keepdims=True)
            zn = (z - mu) * jax.lax.rsqrt(var + EPS)
            zn = zn * gamma.reshape(1, -1, 1) + beta.reshape(1, -1, 1)
            return jax.nn.sigmoid(jax.nn.relu(zn))
        key = jax.random.key(seed)
        k1, k2, k3 = jax.random.split(key, 3)
        B, C, L = (32, 128, 2048)
        x = jax.random.normal(k1, (B, C, L), dtype=jnp.float32)
        channel_map = jax.random.normal(k2, (B, C, L), dtype=jnp.float32)
        fan_in = 2 * 7
        bound = 1.0 / math.sqrt(fan_in)
        conv_w = jax.random.uniform(k3, (1, 2, 7), jnp.float32, -bound, bound)
        bn_gamma = jnp.ones((1,), jnp.float32)
        bn_beta = jnp.zeros((1,), jnp.float32)
        return {'x': x, 'channel_map': channel_map, 'conv_w': conv_w, 'bn_gamma': bn_gamma, 'bn_beta': bn_beta}
    _L0_xattn_all = _L0_xattn_setup()
    _L0_xattn_in = {k: v for k, v in _L0_xattn_all.items() if k in ('conv_w', 'bn_gamma', 'bn_beta')}
    del _L0_xattn_all

    def _L0_attn_setup():
        import jax, jax.numpy as jnp
        import numpy as np
        DIM = 2048
        N_HEADS = 32
        N_KV_HEADS = 8
        HEAD_DIM = DIM // N_HEADS
        N_REP = N_HEADS // N_KV_HEADS
        THETA = 10000.0
        B, S = (4, 512)

        def _rope_cos_sin(seq_len):
            freqs = 1.0 / THETA ** (jnp.arange(0, HEAD_DIM, 2, dtype=jnp.float32) / HEAD_DIM)
            t = jnp.arange(seq_len, dtype=jnp.float32)
            ang = jnp.outer(t, freqs)
            return (jnp.cos(ang), jnp.sin(ang))

        def _apply_rope(x, cos, sin):
            xr = x[..., 0::2]
            xi = x[..., 1::2]
            c = cos[None, :, None, :]
            s = sin[None, :, None, :]
            out_r = xr * c - xi * s
            out_i = xr * s + xi * c
            return jnp.stack([out_r, out_i], axis=-1).reshape(x.shape)
        key = jax.random.key(seed)
        ks = jax.random.split(key, 5)
        sc = 1.0 / np.sqrt(DIM).astype(np.float32)
        x = jax.random.normal(ks[0], (B, S, DIM), jnp.float32)
        wq = jax.random.normal(ks[1], (DIM, N_HEADS * HEAD_DIM), jnp.float32) * sc
        wk = jax.random.normal(ks[2], (DIM, N_KV_HEADS * HEAD_DIM), jnp.float32) * sc
        wv = jax.random.normal(ks[3], (DIM, N_KV_HEADS * HEAD_DIM), jnp.float32) * sc
        wo = jax.random.normal(ks[4], (N_HEADS * HEAD_DIM, DIM), jnp.float32) * sc
        return {'x': x, 'wq': wq, 'wk': wk, 'wv': wv, 'wo': wo}
    _L0_attn_all = _L0_attn_setup()
    _L0_attn_in = {k: v for k, v in _L0_attn_all.items() if k in ('wq', 'wk', 'wv', 'wo')}
    del _L0_attn_all

    def _L0_ffn_setup():
        import jax, jax.numpy as jnp
        import numpy as np
        B, S, D_IN, D_OUT = (2, 1024, 2048, 2048)
        E, K, R = (8, 2, 16)
        SCALING = 32.0 / 16.0
        key = jax.random.key(seed)
        ks = jax.random.split(key, 6)
        x = jax.random.normal(ks[0], (B, S, D_IN), dtype=jnp.float32)
        gate_w = jax.random.normal(ks[1], (E, D_IN), dtype=jnp.float32) * 0.02
        base_w = jax.random.normal(ks[2], (D_OUT, D_IN), dtype=jnp.float32) * 0.02
        base_b = jax.random.normal(ks[3], (D_OUT,), dtype=jnp.float32) * 0.02
        lora_A = jax.random.normal(ks[4], (E, R, D_IN), dtype=jnp.float32) * 0.02
        lora_B = jax.random.normal(ks[5], (E, D_OUT, R), dtype=jnp.float32) * 0.02
        return {'x': x, 'gate_w': gate_w, 'base_w': base_w, 'base_b': base_b, 'lora_A': lora_A, 'lora_B': lora_B}
    _L0_ffn_all = _L0_ffn_setup()
    _L0_ffn_in = {k: v for k, v in _L0_ffn_all.items() if k in ('gate_w', 'base_w', 'base_b', 'lora_A', 'lora_B')}
    del _L0_ffn_all
    return {'x': x, 'ctx_4096': ctx_4096, 'L0_xattn_conv_w': _L0_xattn_in['conv_w'], 'L0_xattn_bn_gamma': _L0_xattn_in['bn_gamma'], 'L0_xattn_bn_beta': _L0_xattn_in['bn_beta'], 'L0_attn_wq': _L0_attn_in['wq'], 'L0_attn_wk': _L0_attn_in['wk'], 'L0_attn_wv': _L0_attn_in['wv'], 'L0_attn_wo': _L0_attn_in['wo'], 'L0_ffn_gate_w': _L0_ffn_in['gate_w'], 'L0_ffn_base_w': _L0_ffn_in['base_w'], 'L0_ffn_base_b': _L0_ffn_in['base_b'], 'L0_ffn_lora_A': _L0_ffn_in['lora_A'], 'L0_ffn_lora_B': _L0_ffn_in['lora_B']}

def reference(x, ctx_4096, L0_xattn_conv_w, L0_xattn_bn_gamma, L0_xattn_bn_beta, L0_attn_wq, L0_attn_wk, L0_attn_wv, L0_attn_wo, L0_ffn_gate_w, L0_ffn_base_w, L0_ffn_base_b, L0_ffn_lora_A, L0_ffn_lora_B):
    import jax
    import jax.numpy as jnp

    def _L0_xattn_ref(x, channel_map, conv_w, bn_gamma, bn_beta):
        import jax, jax.numpy as jnp
        import numpy as np
        import math
        EPS = 1e-05
        LAMBDA = 0.6

        def _crucial_k(C):
            f = math.floor(LAMBDA * C)
            return f + f % 2

        def _conv1d(y, w):
            return jax.lax.conv_general_dilated(y, w, window_strides=(1,), padding=((3, 3),), dimension_numbers=('NCH', 'OIH', 'NCH'))

        def _norm_active(z, gamma, beta):
            mu = jnp.mean(z, axis=(0, 2), keepdims=True)
            var = jnp.mean((z - mu) ** 2, axis=(0, 2), keepdims=True)
            zn = (z - mu) * jax.lax.rsqrt(var + EPS)
            zn = zn * gamma.reshape(1, -1, 1) + beta.reshape(1, -1, 1)
            return jax.nn.sigmoid(jax.nn.relu(zn))
        B, C, L = x.shape
        k = _crucial_k(C)
        cm = jnp.moveaxis(channel_map, 1, 2)
        _, topk_idx = jax.lax.top_k(cm, k)
        b_idx = jnp.arange(B)[:, None, None]
        l_idx = jnp.arange(L)[None, :, None]
        mask = jnp.zeros((B, L, C), x.dtype).at[b_idx, l_idx, topk_idx].set(1.0)
        crucial_channels = jnp.moveaxis(mask, 2, 1)
        subcrucial_channels = 1.0 - crucial_channels
        crucial_features = crucial_channels * x
        subcrucial_features = subcrucial_channels * x
        c_max = jnp.max(crucial_features, axis=1, keepdims=True)
        c_avg = jnp.mean(crucial_features, axis=1, keepdims=True) * (C / k)
        s_max = jnp.max(subcrucial_features, axis=1, keepdims=True)
        s_avg = jnp.mean(subcrucial_features, axis=1, keepdims=True) * (C / (C - k))
        crucial_x = jnp.concatenate([c_max, c_avg], axis=1)
        subcrucial_x = jnp.concatenate([s_max, s_avg], axis=1)
        A_S1 = _norm_active(_conv1d(crucial_x, conv_w), bn_gamma, bn_beta)
        A_S2 = _norm_active(_conv1d(subcrucial_x, conv_w), bn_gamma, bn_beta)
        return crucial_features * A_S1 + subcrucial_features * A_S2

    def _L0_attn_ref(x, wq, wk, wv, wo):
        import jax, jax.numpy as jnp
        import numpy as np
        DIM = 2048
        N_HEADS = 32
        N_KV_HEADS = 8
        HEAD_DIM = DIM // N_HEADS
        N_REP = N_HEADS // N_KV_HEADS
        THETA = 10000.0
        B, S = (4, 512)

        def _rope_cos_sin(seq_len):
            freqs = 1.0 / THETA ** (jnp.arange(0, HEAD_DIM, 2, dtype=jnp.float32) / HEAD_DIM)
            t = jnp.arange(seq_len, dtype=jnp.float32)
            ang = jnp.outer(t, freqs)
            return (jnp.cos(ang), jnp.sin(ang))

        def _apply_rope(x, cos, sin):
            xr = x[..., 0::2]
            xi = x[..., 1::2]
            c = cos[None, :, None, :]
            s = sin[None, :, None, :]
            out_r = xr * c - xi * s
            out_i = xr * s + xi * c
            return jnp.stack([out_r, out_i], axis=-1).reshape(x.shape)
        bsz, seq_len, _ = x.shape
        q = (x @ wq).reshape(bsz, seq_len, N_HEADS, HEAD_DIM)
        k = (x @ wk).reshape(bsz, seq_len, N_KV_HEADS, HEAD_DIM)
        v = (x @ wv).reshape(bsz, seq_len, N_KV_HEADS, HEAD_DIM)
        cos, sin = _rope_cos_sin(seq_len)
        q = _apply_rope(q, cos, sin)
        k = _apply_rope(k, cos, sin)
        k = jnp.repeat(k, N_REP, axis=2)
        v = jnp.repeat(v, N_REP, axis=2)
        scores = jnp.einsum('bqhd,bkhd->bhqk', q, k) / np.float32(np.sqrt(HEAD_DIM))
        mask = jnp.triu(jnp.full((seq_len, seq_len), -jnp.inf, dtype=scores.dtype), k=1)
        scores = scores + mask
        attn = jax.nn.softmax(scores.astype(jnp.float32), axis=-1).astype(q.dtype)
        out = jnp.einsum('bhqk,bkhd->bqhd', attn, v).reshape(bsz, seq_len, N_HEADS * HEAD_DIM)
        return out @ wo

    def _L0_ffn_ref(x, gate_w, base_w, base_b, lora_A, lora_B):
        import jax, jax.numpy as jnp
        import numpy as np
        B, S, D_IN, D_OUT = (2, 1024, 2048, 2048)
        E, K, R = (8, 2, 16)
        SCALING = 32.0 / 16.0
        gate_logits = jnp.einsum('bsd,ed->bse', x, gate_w)
        weights, selected = jax.lax.top_k(gate_logits, K)
        weights = jax.nn.softmax(weights.astype(jnp.float32), axis=2).astype(x.dtype)
        result = jnp.einsum('bsd,od->bso', x, base_w) + base_b
        w_full = jnp.sum(jax.nn.one_hot(selected, E, dtype=x.dtype) * weights[..., None], axis=2)
        low = jnp.einsum('bsd,erd->ebsr', x, lora_A)
        lora_out = jnp.einsum('ebsr,eor,bse->bso', low, lora_B, w_full)
        result = result + SCALING * lora_out
        return result
    x = x + _L0_xattn_ref(_layernorm(x, axis=-1), ctx_4096, L0_xattn_conv_w, L0_xattn_bn_gamma, L0_xattn_bn_beta)
    x = x + _L0_attn_ref(_layernorm(x, axis=-1), L0_attn_wq, L0_attn_wk, L0_attn_wv, L0_attn_wo)
    x = x + _L0_ffn_ref(_layernorm(x, axis=-1), L0_ffn_gate_w, L0_ffn_base_w, L0_ffn_base_b, L0_ffn_lora_A, L0_ffn_lora_B)
    return x

_drawn_inputs = setup_inputs


def setup_inputs(seed=0):
    import zlib

    import numpy as np

    out = dict(_drawn_inputs(seed))
    spreads = {}
    factors = {'L0_ffn_base_b': 5.493}
    for name, (base, spread) in spreads.items():
        noise = np.random.default_rng([zlib.crc32(name.encode()), seed]).standard_normal(out[name].shape)
        drawn = base * np.exp(spread * noise) if base else spread * noise
        out[name] = jnp.asarray(drawn.astype(out[name].dtype))
    for name, factor in factors.items():
        out[name] = (out[name] * factor).astype(out[name].dtype)
    return out
```

```python
import numpy as np
import concourse.bass as bass
import concourse.mybir as mybir

F32 = mybir.dt.float32
F32R = mybir.dt.float32r
BF16 = mybir.dt.bfloat16
ALU = mybir.AluOpType
ACT = mybir.ActivationFunctionType
AX = mybir.AxisListType

B, C, L, CM = 16, 64, 2048, 1601
K = 38
NT = 16
HT = 512
HB = 8
EPS = 1e-5
NEG = -1.0e30

C_ONES, C_SHL, C_SHR, C_ID, C_MASK, C_COS, C_SIN, C_TRI, C_SEL, C_END = 0, 128, 256, 384, 512, 640, 704, 768, 832, 960


def constants():
    c = np.zeros((128, C_END), np.float32)
    c[:, C_ONES:C_ONES + 128] = 1.0
    for p in range(128):
        if p >= 1:
            c[p - 1, C_SHL + p] = 1.0
        if p <= 126:
            c[p + 1, C_SHR + p] = 1.0
        c[p, C_ID + p] = 1.0
    q = np.arange(128)
    ok = (q[:, None] // 64 == q[None, :] // 64) & (q[None, :] <= q[:, None])
    c[:, C_MASK:C_MASK + 128] = np.where(ok, 0.0, NEG)
    freqs = (np.float32(1.0) / np.float32(10000.0) ** (np.arange(0, 64, 2, dtype=np.float32) / np.float32(64))).astype(np.float32)
    ang = np.outer(np.arange(64, dtype=np.float32), freqs).astype(np.float32)
    d = q % 64
    c[:, C_COS:C_COS + 64] = np.cos(ang)[:, d // 2].T
    c[:, C_SIN:C_SIN + 64] = np.where(d % 2 == 0, -1.0, 1.0)[:, None] * np.sin(ang)[:, d // 2].T
    e = np.arange(8)
    c[:, C_TRI:C_TRI + 64] = (e[None, :] < e[:, None]).astype(np.float32).reshape(1, 64)
    for k in range(8):
        c[k, C_SEL + 16 * k:C_SEL + 16 * k + 16] = 1.0
    return c


class Queues:

    def __init__(self, nc):
        self.nc = nc
        self.q = {n: [] for n in ("vector", "scalar", "gpsimd", "tensor", "sync")}
        self.sem = {n: nc.alloc_semaphore("s_" + n) for n in ("vector", "scalar", "gpsimd", "tensor")}
        self.count = {n: 0 for n in self.sem}
        self.dcount = {}

    def op(self, eng, fn, waits):
        self.count[eng] += 1
        self.q[eng].append((waits, fn, self.sem[eng], 1))
        return (self.sem[eng], self.count[eng])

    def V(self, fn, *w):
        return self.op("vector", fn, w)

    def A(self, fn, *w):
        return self.op("scalar", fn, w)

    def P(self, fn, *w):
        return self.op("gpsimd", fn, w)

    def T(self, fn, *w):
        return self.op("tensor", fn, w)

    def D(self, eng, sem, out, in_, *w):
        self.dcount[sem] = self.dcount.get(sem, 0) + 16
        self.q[eng].append((w, lambda e: e.dma_start(out, in_), sem, 16))
        return (sem, self.dcount[sem])

    def emit(self, eng, e):
        seen = {}
        for waits, fn, sem, inc in self.q[eng]:
            for t in waits:
                if t is not None and seen.get(t[0], 0) < t[1]:
                    e.wait_ge(t[0], t[1])
                    seen[t[0]] = t[1]
            if fn is not None:
                fn(e).then_inc(sem, inc)


def build(nc, ctxT, xT, cw, bn, cst_d, wqkv, wo, wl, wb, gw, bb, out):
    Q = Queues(nc)
    V, A, P, T = Q.V, Q.A, Q.P, Q.T
    x1d = nc.dram_tensor("x1d", [128, 2, NT, HT], F32).ap()
    x2d = nc.dram_tensor("x2d", [128, 2, NT, HT], F32).ap()
    base = (nc.sbuf_base + 63) // 64 * 64
    names = [0]

    def at(off, shape, dt=F32):
        names[0] += 1
        return nc.alloc_sbuf_tensor_at(f"t{names[0]}", [128] + shape, dt, offset=base + off)

    KB = 1024
    top = [128 * KB]

    def sb(shape, dt=F32):
        n = 1
        for s in shape:
            n *= s
        n *= 2 if dt == BF16 else 4
        off = top[0]
        top[0] += (n + 31) // 32 * 32
        return at(off, shape, dt)

    def sem(n):
        return nc.alloc_semaphore(n)

    XN = at(0, [2, NT, HT])
    ATH = at(0, [NT, HT], F32R)
    ATL = at(32 * KB, [NT, HT], F32R)
    AF0 = at(0, [NT, HT])
    AF1 = at(32 * KB, [NT, HT])
    XF0 = at(64 * KB, [NT, HT])
    XF1 = at(96 * KB, [NT, HT])
    XL_ = at(64 * KB, [NT, HT], F32R)
    XH_ = at(96 * KB, [NT, HT], F32R)
    AL_ = ATL
    NR = 3
    RS = (2 * CM * 4 + 63) // 64 * 64
    ring = [at(64 * KB + i * RS, [2, CM]) for i in range(NR)]
    o = 64 * KB + NR * RS
    o = (o + 63) // 64 * 64
    crc = at(o, [NT, C]); o += 4096
    sbc = at(o, [NT, C]); o += 4096
    tk = at(o, [2, 40]); o += 320
    cnd = at(o, [2, C]); o += 512
    gtb = at(o, [C]); o += 256
    eqb = at(o, [C]); o += 256
    prb = at(o, [C]); o += 256
    sm = at(o, [8]); o += 64
    assert o <= 128 * KB

    mask_off = top[0]
    kT = sb([4, HT])
    Vt = sb([4, HT])
    SB = [sb([HT]) for _ in range(2)]
    PTs = [sb([HT]) for _ in range(2)]
    qr_off = top[0]
    qr = [sb([HT]) for _ in range(2)]
    qs_off = top[0]
    qs = sb([HT])
    t1 = sb([HT])
    assert top[0] - mask_off >= 32 * KB
    mask = at(mask_off, [B, NT, C], BF16)
    raw = [sb([4, 128]) for _ in range(3)]
    wh = [sb([4, 128], F32R) for _ in range(4)]
    wlo = [sb([4, 128], F32R) for _ in range(4)]
    cst = sb([C_END])
    Mn = sb([HT])
    Rs = sb([HT])
    R1 = sb([HT])
    tx_off = top[0]
    rc = [sb([HT]) for _ in range(2)]
    ev = [sb([HT]) for _ in range(2)]
    stat_off = top[0]
    stat = sb([4, B, NT])
    lgh = at(stat_off, [HT], F32R)
    lgl = at(stat_off + 2 * KB, [HT], F32R)
    t2 = at(qs_off, [HT])
    gwr = sb([NT, 8])
    gwh = sb([NT, 8], F32R)
    gwl = sb([NT, 8], F32R)
    bbs = sb([NT])
    w16 = sb([16])
    sc = sb([160])
    assert top[0] <= nc.sbuf_usable_end - base, top[0]
    Yp = at(64 * KB, [4 * B, 22])
    Z = at(64 * KB + 4 * B * 22 * 4, [2, 256])
    Zt = at(64 * KB + 4 * B * 22 * 4 + 2048, [2, 256])
    A12 = at(64 * KB + 4 * B * 22 * 4 + 4096, [2, 256])
    Dm = stat[:, 0, :, :]
    A2 = stat[:, 1, :, :]
    tx = [at(tx_off + 4096 * i, [NT, C]) for i in range(2)]

    ps = [nc.alloc_psum_tensor(f"ps{i}", [128, 512], F32) for i in range(8)]
    PA, PS_, PT, PO = ps[0:3], ps[3:5], ps[5:7], ps[7]

    d_c = sem("d_c"); d_x = [sem("d_x0"), sem("d_x1")]
    d_r = [sem(f"d_r{i}") for i in range(NR)]
    d_w = [sem(f"d_w{i}") for i in range(3)]
    d_xr = [sem("d_xr0"), sem("d_xr1")]
    d_s = sem("d_s"); d_s2 = sem("d_s2"); d_rc = [sem("d_rc0"), sem("d_rc1")]
    d_o = [sem("d_o0"), sem("d_o1")]
    d_ln = sem("d_ln")

    ones = cst[:, C_ONES:C_ONES + 128]
    ident = cst[:, C_ID:C_ID + 128]

    k_c = Q.D("sync", d_c, cst[:, :], cst_d)
    k_c = Q.D("sync", d_c, w16[:, 0:14], cw)
    k_c = Q.D("sync", d_c, w16[:, 14:16], bn)
    k_c = Q.D("sync", d_c, bbs[:, :], bb)
    k_c = Q.D("sync", d_c, gwr[:, :, :], gw)
    k_x = [Q.D("sync", d_x[h], XN[:, h, :, :], xT[:, h, :, :]) for h in range(2)]

    def over_t(ap):
        return ap.rearrange("p t n -> p n t")

    def bc(ap, n):
        return ap.rearrange("p (a n) -> p a n", a=1).to_broadcast([128, n, HT])

    def layernorm(x, scratch, bank, waits, bank_free):
        k = V(lambda e: e.tensor_reduce(R1[:, :], over_t(x[:, :, :]), AX.X, ALU.add), *waits)
        k = T(lambda e: e.matmul(bank[:, :], ones, R1[:, :], start=True, stop=True), k, bank_free, k_c)
        k = V(lambda e: e.tensor_scalar(Mn[:, :], bank[:, :], 1.0 / L, None, ALU.mult), k)
        a = V(lambda e: e.tensor_tensor(x[:, 0:11, :], x[:, 0:11, :], bc(Mn[:, :], 11), ALU.subtract), k)
        b = P(lambda e: e.tensor_tensor(x[:, 11:16, :], x[:, 11:16, :], bc(Mn[:, :], 5), ALU.subtract), k)
        k1 = A(lambda e: e.activation(scratch[:, 0:11, :], x[:, 0:11, :], ACT.Square), a)
        k2 = A(lambda e: e.activation(scratch[:, 11:16, :], x[:, 11:16, :], ACT.Square), b)
        k = V(lambda e: e.tensor_reduce(R1[:, :], over_t(scratch[:, :, :]), AX.X, ALU.add), k1, k2)
        k = T(lambda e: e.matmul(bank[:, :], ones, R1[:, :], start=True, stop=True), k)
        k = V(lambda e: e.tensor_scalar(Mn[:, :], bank[:, :], 1.0 / L, EPS, ALU.mult, ALU.add), k)
        bf = k
        k = A(lambda e: e.activation(R1[:, :], Mn[:, :], ACT.Sqrt), k)
        k = V(lambda e: e.reciprocal(Rs[:, :], R1[:, :]), k)
        return k, bf

    k_xn = []
    bf = None
    for h in range(2):
        x = XN[:, h, :, :]
        k, bf = layernorm(x, (XF0 if h == 0 else XF1)[:, :, :], PA[0], [k_x[h]] + k_xn, bf)
        a = V(lambda e, x=x: e.tensor_tensor(x[:, 0:11, :], x[:, 0:11, :], bc(Rs[:, :], 11), ALU.mult), k)
        b = P(lambda e, x=x: e.tensor_tensor(x[:, 11:16, :], x[:, 11:16, :], bc(Rs[:, :], 5), ALU.mult), k)
        k_xn += [a, b]

    freed = [None] * NR
    free_all = None
    k_prev = k_xn[-2]
    k_cs = None
    k_tile = None
    for b in range(B):
        for tp in range(8):
            s = (b * 8 + tp) % NR
            k_l = Q.D("sync", d_r[s], ring[s][:, :, :],
                      ctxT[b].rearrange("(p t) c -> p t c", t=NT)[:, 2 * tp:2 * tp + 2, :], freed[s], *k_xn)
            for u in range(2):
                t = 2 * tp + u
                r = ring[s][:, u, :]
                kc = A(lambda e, r=r, u=u: e.activation(cnd[:, u, :], r[:, 0:C], ACT.Copy), k_l, k_tile)
                k = kc
                for i in range(5):
                    k = V(lambda e, r=r, i=i, u=u: e.max(tk[:, u, 8 * i:8 * i + 8], r), k, k_l)
                    if i < 4:
                        k = V(lambda e, r=r, i=i, u=u: e.match_replace(r, tk[:, u, 8 * i:8 * i + 8], r, -3.0e38), k)
                freed[s] = k
                thr = tk[:, u, K - 1:K]
                k = V(lambda e, thr=thr, u=u: e.tensor_scalar(prb[:, 0:40], tk[:, u, :], thr, None, ALU.is_gt, ALU.add,
                                                         accum_out=sm[:, 0:1]), k)
                k = V(lambda e: e.tensor_scalar(sm[:, 1:2], sm[:, 0:1], -1.0, float(K), ALU.mult, ALU.add), k)
                k = V(lambda e, thr=thr, u=u: e.tensor_scalar(eqb[:, :], cnd[:, u, :], thr, None, ALU.is_equal), k)
                k = V(lambda e, thr=thr, u=u: e.tensor_scalar(gtb[:, :], cnd[:, u, :], thr, None, ALU.is_gt), k)
                k = V(lambda e: e.tensor_tensor_scan(prb[:, :], cst[:, C_ONES:C_ONES + C], eqb[:, :], 0.0,
                                                     ALU.mult, ALU.add), k)
                k = V(lambda e: e.scalar_tensor_tensor(prb[:, :], prb[:, :], sm[:, 1:2], eqb[:, :],
                                                       ALU.is_le, ALU.mult), k)
                k = V(lambda e, b=b, t=t: e.tensor_tensor(mask[:, b, t, :], prb[:, :], gtb[:, :], ALU.add), k)
                k_tile = k
        xb = XN[:, b // HB, :, (b % HB) * C:(b % HB) * C + C]
        mb = mask[:, b, :, :]
        k1 = P(lambda e, xb=xb, mb=mb: e.tensor_tensor(crc[:, :, :], mb, xb, ALU.mult), k_tile, k_cs)
        k2 = P(lambda e, xb=xb: e.tensor_tensor(sbc[:, :, :], xb, crc[:, :, :], ALU.subtract), k1)
        V(lambda e, b=b: e.tensor_reduce(stat[:, 0, b, :], crc[:, :, :], AX.X, ALU.max), k1)
        V(lambda e, b=b: e.tensor_reduce(stat[:, 1, b, :], sbc[:, :, :], AX.X, ALU.max), k2)
        V(lambda e, b=b: e.tensor_reduce(stat[:, 2, b, :], crc[:, :, :], AX.X, ALU.add), k1)
        k_cs = V(lambda e, b=b: e.tensor_reduce(stat[:, 3, b, :], sbc[:, :, :], AX.X, ALU.add), k2)
    k_ph1 = k_cs

    Y4 = Yp[:, :, :].rearrange("p (f b) t -> p f b t", f=4)
    k = V(lambda e: e.tensor_scalar(stat[:, 2, :, :], stat[:, 2, :, :], 1.0 / C, C / K, ALU.mult, ALU.mult), k_cs)
    k = V(lambda e: e.tensor_scalar(stat[:, 3, :, :], stat[:, 3, :, :], 1.0 / C, C / (C - K), ALU.mult, ALU.mult), k)
    st = stat[:, :, :, :].rearrange("p f b t -> p (f b) t")
    kk = V(lambda e: e.tensor_copy(Yp[:, :, 3:19], st), k)
    kl = T(lambda e: e.matmul(PA[1][:, 0:192].rearrange("p (g t) -> p g t", t=3), cst[:, C_SHL:C_SHL + 128],
                              st[:, :, 13:16], start=True, stop=True), k)
    kr = T(lambda e: e.matmul(PA[2][:, 0:192].rearrange("p (g t) -> p g t", t=3), cst[:, C_SHR:C_SHR + 128],
                              st[:, :, 0:3], start=True, stop=True), k)
    kl = V(lambda e: e.tensor_copy(Yp[:, :, 0:3], PA[1][:, 0:192].rearrange("p (g t) -> p g t", t=3)), kl)
    k = V(lambda e: e.tensor_copy(Yp[:, :, 19:22], PA[2][:, 0:192].rearrange("p (g t) -> p g t", t=3)), kr)
    Zf = Z[:, :, :].rearrange("p s (b t) -> p (s b) t", t=NT)
    for ch in range(2):
        for tap in range(7):
            src = Yp[:, ch * 32:ch * 32 + 32, tap:tap + 16]
            wsc = w16[:, ch * 7 + tap:ch * 7 + tap + 1]
            if ch == 0 and tap == 0:
                k = V(lambda e, src=src, wsc=wsc: e.tensor_scalar(Zf, src, wsc, None, ALU.mult), k, k_c)
            else:
                k = V(lambda e, src=src, wsc=wsc: e.scalar_tensor_tensor(Zf, src, wsc, Zf, ALU.mult, ALU.add), k)

    def total(src, col):
        k1 = V(lambda e: e.tensor_reduce(sc[:, col + 2:col + 4], src, AX.X, ALU.add), k)
        k2 = T(lambda e: e.matmul(PA[1][:, 0:2], ones, sc[:, col + 2:col + 4], start=True, stop=True), k1)
        return V(lambda e: e.tensor_scalar(sc[:, col:col + 2], PA[1][:, 0:2], 1.0 / (B * L), None, ALU.mult), k2)

    k = total(Z[:, :, :], 0)
    for s in range(2):
        k = V(lambda e, s=s: e.tensor_scalar(Z[:, s, :], Z[:, s, :], sc[:, s:s + 1], None, ALU.subtract), k)
    k = V(lambda e: e.tensor_tensor(Zt[:, :, :], Z[:, :, :], Z[:, :, :], ALU.mult), k)
    k = total(Zt[:, :, :], 4)
    k = V(lambda e: e.tensor_scalar(sc[:, 8:10], sc[:, 4:6], EPS, None, ALU.add), k)
    k = A(lambda e: e.activation(sc[:, 10:12], sc[:, 8:10], ACT.Sqrt), k)
    k = V(lambda e: e.reciprocal(sc[:, 12:14], sc[:, 10:12]), k)
    for s in range(2):
        k = V(lambda e, s=s: e.tensor_scalar(Z[:, s, :], Z[:, s, :], sc[:, 12 + s:13 + s], w16[:, 14:15],
                                             ALU.mult, ALU.mult), k)
    k = V(lambda e: e.tensor_scalar(Z[:, :, :], Z[:, :, :], w16[:, 15:16], 0.0, ALU.add, ALU.max), k)
    k = A(lambda e: e.activation(Zt[:, :, :], Z[:, :, :], ACT.Exp, scale=-1.0), k)
    k = V(lambda e: e.tensor_scalar(Zt[:, :, :], Zt[:, :, :], 1.0, None, ALU.add), k)
    k = V(lambda e: e.reciprocal(A12[:, :, :], Zt[:, :, :]), k)
    k = V(lambda e: e.tensor_tensor(Dm, A12[:, 0, :].rearrange("p (b t) -> p b t", t=NT),
                                    A12[:, 1, :].rearrange("p (b t) -> p b t", t=NT), ALU.subtract), k)
    k_g = V(lambda e: e.tensor_copy(A2, A12[:, 1, :].rearrange("p (b t) -> p b t", t=NT)), k)

    k_xr = [Q.D("sync", d_xr[h], (XF0, XF1)[h][:, :, :], xT[:, h, :, :], k_g) for h in range(2)]
    last = None
    k_x1 = []
    free = [None, None]
    for b in range(B):
        h = b // HB
        xr = (XF0, XF1)[h][:, :, (b % HB) * C:(b % HB) * C + C]
        xb = XN[:, h, :, (b % HB) * C:(b % HB) * C + C]
        dm = Dm[:, b, :].rearrange("p (t a) -> p t a", a=1).to_broadcast([128, NT, C])
        a2 = A2[:, b, :].rearrange("p (t a) -> p t a", a=1).to_broadcast([128, NT, C])
        u = tx[b % 2][:, :, :]
        mb = mask[:, b, :, :]
        k = V(lambda e, u=u, mb=mb, dm=dm: e.tensor_tensor(u, mb, dm, ALU.mult), k_g, free[b % 2])
        k = V(lambda e, u=u, a2=a2: e.tensor_tensor(u, u, a2, ALU.add), k)
        k = P(lambda e, u=u, xb=xb: e.tensor_tensor(u, u, xb, ALU.mult), k)
        if last:
            lu, lx, lk, lh, lb = last
            free[lb] = V(lambda e, lu=lu, lx=lx: e.tensor_tensor(lx, lx, lu, ALU.add), lk, k_xr[lh])
            if b == HB:
                k_x1.append(free[lb])
        last = (u, xr, k, h, b % 2)
    lu, lx, lk, lh, lb = last
    k_x1.append(V(lambda e: e.tensor_tensor(lx, lx, lu, ALU.add), lk, k_xr[1]))
    k_sx1 = [Q.D("sync", d_s, x1d[:, h, :, :], (XF0, XF1)[h][:, :, :], k_x1[h]) for h in range(2)]
    k_sx1 = k_sx1[1]

    NH_ = len(wh)
    wst = {"n": 0, "raw": [None] * 3, "wf": [None] * NH_}

    def chunk(src, nk):
        n = wst["n"]
        wst["n"] += 1
        r, s = n % 3, n % NH_
        k = Q.D("sync", d_w[r], raw[r][:, 0:nk, :], src, wst["raw"][r])
        rr, hh, ll = raw[r][:, 0:nk, :], wh[s][:, 0:nk, :], wlo[s][:, 0:nk, :]
        k = A(lambda e: e.activation(hh, rr, ACT.Copy), k, wst["wf"][s])
        k = P(lambda e: e.tensor_tensor(ll, rr, hh.bitcast(F32), ALU.subtract), k, wst["wf"][s])
        wst["raw"][r] = k
        return s, k

    pend = []

    def order(items):
        for it in items:
            pend.append(it)

    AHEAD = 2
    ready = []

    def feed():
        while pend and len(ready) < AHEAD + 1:
            ready.append(chunk(*pend.pop(0)))

    pa_free = [None] * 3
    pan = [0]

    def project(X, xk, extra=None):
        i = pan[0] % 3
        pan[0] += 1
        bank = PA[i]
        XHx, XLx = X
        total_ = 4 + (1 if extra else 0)
        for c in range(total_):
            feed()
            s, kw = ready.pop(0)
            nk = 4 if c < 4 else 1

            def fn(e, c=c, s=s, nk=nk):
                for q in range(nk):
                    kt = 4 * c + q
                    xh, xl = (XHx[:, kt, :], XLx[:, kt, :]) if c < 4 else (extra[0][:, :], extra[1][:, :])
                    e.matmul(bank[:, :], wh[s][:, q, :], xl, start=(c == 0 and q == 0), stop=False)
                    e.matmul(bank[:, :], wlo[s][:, q, :], xh, start=False, stop=False)
                    m = e.matmul(bank[:, :], wh[s][:, q, :], xh, start=False, stop=(c == total_ - 1 and q == nk - 1))
                return m
            k = T(fn, kw, *(xk if c == 0 else []), pa_free[i] if c == 0 else None, extra[2] if c == 4 else None)
            wst["wf"][s] = k
        return i, bank, k

    def wblock(w, nb, extra=False):
        src = w[nb]
        out_ = [(src[:, 4 * c:4 * c + 4, :], 4) for c in range(4)]
        if extra:
            out_.append((src[:, 16:17, :], 1))
        return out_

    def lnsplit(x, scratch, hi, lo_, waits):
        i = pan[0] % 3
        pan[0] += 1
        k, bf_ = layernorm(x, scratch, PA[i], waits, pa_free[i])
        pa_free[i] = bf_
        a = V(lambda e: e.tensor_tensor(x[:, 0:11, :], x[:, 0:11, :], bc(Rs[:, :], 11), ALU.mult), k)
        b_ = P(lambda e: e.tensor_tensor(x[:, 11:16, :], x[:, 11:16, :], bc(Rs[:, :], 5), ALU.mult), k)
        a1 = A(lambda e: e.activation(hi[:, 0:8, :], x[:, 0:8, :], ACT.Copy), a)
        a2_ = A(lambda e: e.activation(hi[:, 8:16, :], x[:, 8:16, :], ACT.Copy), a, b_)
        V(lambda e: e.tensor_tensor(lo_[:, 0:8, :], x[:, 0:8, :], hi[:, 0:8, :].bitcast(F32), ALU.subtract), a1)
        return V(lambda e: e.tensor_tensor(lo_[:, 8:16, :], x[:, 8:16, :], hi[:, 8:16, :].bitcast(F32), ALU.subtract), a2_)

    maskc = cst[:, C_MASK:C_MASK + 128].rearrange("p (a n) -> p a n", a=1).to_broadcast([128, 4, 128])
    swap = [i ^ 1 for i in range(32)]

    def rope(dst, bank, k, dst_free):
        cosb = cst[:, C_COS:C_COS + 64].rearrange("p (a n) -> p a n", a=1).to_broadcast([128, 8, 64])
        sinb = cst[:, C_SIN:C_SIN + 64].rearrange("p (a n) -> p a n", a=1).to_broadcast([128, 8, 64])

        def v3(ap):
            return ap.rearrange("p (a n) -> p a n", n=64)
        a = V(lambda e: e.stream_shuffle(qs[:, :], bank[:, :], swap), k, rope_free[0])
        b_ = V(lambda e: e.tensor_tensor(v3(t1[:, :]), v3(bank[:, :]), cosb, ALU.mult), k, rope_free[0])
        c = P(lambda e: e.tensor_tensor(v3(qs[:, :]), v3(qs[:, :]), sinb, ALU.mult), a)
        d = P(lambda e: e.tensor_tensor(dst, t1[:, :], qs[:, :], ALU.add), b_, c, dst_free)
        rope_free[0] = d
        return d, b_

    rope_free = [None]
    st_ = {"S": [None] * 2, "PT": [None] * 2, "O": None, "SB": [None] * 2, "PTs": [None] * 2, "qr": [None] * 2}

    def qk_scores(i, kq, kk_):
        j = i // 4
        toks = []
        for s in range(2):
            def fn(e, s=s):
                for pr in range(4):
                    m = e.matmul(PS_[s][:, pr * 128:pr * 128 + 128],
                                 qr[i % 2][64 * s:64 * s + 64, pr * 128:pr * 128 + 128],
                                 kT[64 * s:64 * s + 64, j, pr * 128:pr * 128 + 128], start=True, stop=True)
                return m
            k = T(fn, kq, kk_, st_["S"][s])
            if s == 1:
                st_["qr"][i % 2] = k
            p3 = SB[s][:, :].rearrange("p (a n) -> p a n", n=128)
            s3 = PS_[s][:, :].rearrange("p (a n) -> p a n", n=128)
            b0 = 16 + s * 16
            k = V(lambda e, p3=p3, s3=s3: e.scalar_tensor_tensor(p3, s3, 0.125, maskc, ALU.mult, ALU.add), k, st_["SB"][s])
            st_["S"][s] = k
            k = V(lambda e, p3=p3, b0=b0: e.tensor_reduce(sc[:, b0:b0 + 4], p3, AX.X, ALU.max), k)
            mx = sc[:, b0:b0 + 4].rearrange("p (a n) -> p a n", n=1).to_broadcast([128, 4, 128])
            k = V(lambda e, p3=p3, mx=mx: e.tensor_tensor(p3, p3, mx, ALU.subtract), k)
            k = A(lambda e, s=s: e.activation(SB[s][:, :], SB[s][:, :], ACT.Exp), k)
            k = V(lambda e, p3=p3, b0=b0: e.tensor_reduce(sc[:, b0 + 4:b0 + 8], p3, AX.X, ALU.add), k)
            k = V(lambda e, b0=b0: e.reciprocal(sc[:, b0 + 8:b0 + 12], sc[:, b0 + 4:b0 + 8]), k)
            rr = sc[:, b0 + 8:b0 + 12].rearrange("p (a n) -> p a n", n=1).to_broadcast([128, 4, 128])
            k = P(lambda e, p3=p3, rr=rr: e.tensor_tensor(p3, p3, rr, ALU.mult), k)
            toks.append(k)
        return toks

    def transpose_p(i, toks):
        out_ = []
        for s in range(2):
            def fn(e, s=s):
                for pr in range(4):
                    m = e.transpose(PT[s][:, pr * 128:pr * 128 + 128], SB[s][:, pr * 128:pr * 128 + 128], ident)
                return m
            k = T(fn, toks[s], st_["PT"][s])
            st_["SB"][s] = k
            k = A(lambda e, s=s: e.activation(PTs[s][:, :], PT[s][:, :], ACT.Copy), k, st_["PTs"][s])
            st_["PT"][s] = k
            out_.append(k)
        return out_

    def times_v(i, toks, kv, at_free):
        j = i // 4

        def fn(e, s):
            for pr in range(4):
                m = e.matmul(PO[64 * s:64 * s + 64, pr * 128:pr * 128 + 128],
                             Vt[:, pr, (2 * j + s) * 64:(2 * j + s) * 64 + 64],
                             PTs[s][:, pr * 128:pr * 128 + 128], start=True, stop=True)
            return m
        for s in range(2):
            k = T(lambda e, s=s: fn(e, s), toks[s], kv, st_["O"] if s == 0 else None)
            st_["PTs"][s] = k
        a = A(lambda e: e.activation(ATH[:, i, :], PO[:, :], ACT.Copy), k, at_free)
        b_ = V(lambda e: e.tensor_tensor(ATL[:, i, :], PO[:, :], ATH[:, i, :].bitcast(F32), ALU.subtract), a)
        st_["O"] = b_
        return b_

    def qkv_attention(X, xk, region_free, at_free):
        for nb in range(4):
            order(wblock(wqkv, 16 + nb))
        for nb in range(4):
            order(wblock(wqkv, 20 + nb))
        for nb in range(16):
            order(wblock(wqkv, nb))
        kks = []
        for j in range(4):
            i, bank, k = project(X, xk)
            kd, bf_ = rope(kT[:, j, :], bank, k, region_free)
            pa_free[i] = bf_
            kks.append(kd)
        kvs = []
        vt = None

        def vturn(j, kx):
            def fn(e):
                for tb in range(4):
                    m = e.transpose(PT[j % 2][:, tb * 128:tb * 128 + 128], SB[j % 2][:, tb * 128:tb * 128 + 128], ident)
                return m
            k = T(fn, kx, st_["PT"][j % 2])
            st_["SB"][j % 2] = k
            k = V(lambda e: e.tensor_copy(Vt[:, :, j * 128:j * 128 + 128],
                                          PT[j % 2][:, :].rearrange("p (a n) -> p a n", n=128)), k, region_free)
            st_["PT"][j % 2] = k
            kvs.append(k)
        for j in range(4):
            i, bank, k = project(X, xk)
            kx = V(lambda e, j=j, bank=bank: e.tensor_copy(SB[j % 2][:, :], bank[:, :]), k, st_["SB"][j % 2], region_free)
            pa_free[i] = kx
            if vt:
                vturn(*vt)
            vt = (j, kx)
        sco = {}
        last = None
        for i in range(18):
            if i >= 2:
                pt = transpose_p(i - 2, sco.pop(i - 2))
            if i < 16:
                pi, bank, k = project(X, xk)
                if i == 15:
                    k_x_done = k
                if i == 0:
                    vturn(*vt)
                kq, bf_ = rope(qr[i % 2][:, :], bank, k, st_["qr"][i % 2] or region_free)
                pa_free[pi] = bf_
                kqs = kq if i == 0 else kq
            if i >= 2:
                last = times_v(i - 2, pt, kvs[-1], at_free)
            if i >= 1 and i <= 16:
                sco[i - 1] = qk_scores(i - 1, kprev, kks[-1])
            kprev = kq
        return last, k_x_done

    rcn = [0]
    rc_free = [None, None]
    ev_free = [None, None]

    def wo_half(h, X, xk):
        for nb in range(16):
            order(wblock(wo, nb))
        kst = None
        for nb in range(16):
            s = rcn[0] % 2
            rcn[0] += 1
            kr_ = Q.D("sync", d_rc[s], rc[s][:, :], x1d[:, h, nb, :], rc_free[s], k_sx1)
            i, bank, k = project(X, [xk])
            k = V(lambda e, s=s, bank=bank: e.tensor_tensor(ev[s][:, :], bank[:, :], rc[s][:, :], ALU.add), k, kr_, ev_free[s])
            pa_free[i] = k
            rc_free[s] = k
            ev_free[s] = Q.D("sync", d_o[s], x2d[:, h, nb, :], ev[s][:, :], k)
        return list(ev_free), k

    trib = cst[:, C_TRI:C_TRI + 64].rearrange("p (c j) -> p c j", j=8)

    def gates(X, xk, need):
        XHx, XLx = X
        g = Zg
        i = pan[0] % 3
        pan[0] += 1
        b1 = PA[i]

        def fn(e):
            for tb in range(4):
                for kt in range(16):
                    xh = XHx[:, kt, tb * 128:tb * 128 + 128]
                    xl = XLx[:, kt, tb * 128:tb * 128 + 128]
                    o_ = b1[:, tb * 8:tb * 8 + 8]
                    e.matmul(o_, xl, gwh[:, kt, :], start=(kt == 0), stop=False)
                    e.matmul(o_, xh, gwl[:, kt, :], start=False, stop=False)
                    m = e.matmul(o_, xh, gwh[:, kt, :], start=False, stop=(kt == 15))
            return m
        k = T(fn, xk, k_gw, pa_free[i])
        lg = g[:, 0:32]
        k = V(lambda e: e.tensor_copy(lg, b1[:, 0:32]), k, need)
        pa_free[i] = k
        G4 = g[:, 32:288].rearrange("p (a c j) -> p a c j", c=8, j=8)
        H4 = g[:, 288:544].rearrange("p (a c j) -> p a c j", c=8, j=8)
        for tb in range(4):
            lj = g[:, tb * 8:tb * 8 + 8].rearrange("p (a j) -> p a j", a=1).to_broadcast([128, 8, 8])
            lc = g[:, tb * 8:tb * 8 + 8].rearrange("p (c a) -> p c a", a=1).to_broadcast([128, 8, 8])
            k = V(lambda e, tb=tb, lj=lj, lc=lc: e.tensor_tensor(G4[:, tb, :, :], lj, lc, ALU.is_gt), k)
            k = V(lambda e, tb=tb, lj=lj, lc=lc: e.tensor_tensor(H4[:, tb, :, :], lj, lc, ALU.is_equal), k)
            k = V(lambda e, tb=tb: e.tensor_tensor(H4[:, tb, :, :], H4[:, tb, :, :], trib, ALU.mult), k)
        k = V(lambda e: e.tensor_tensor(g[:, 32:288], g[:, 32:288], g[:, 288:544], ALU.add), k)
        k = V(lambda e: e.tensor_reduce(g[:, 288:320], G4.rearrange("p a c j -> p (a c) j"), AX.X, ALU.add), k)
        k = V(lambda e: e.tensor_scalar(g[:, 288:320], g[:, 288:320], 2.0, None, ALU.is_lt), k)
        l3 = lg.rearrange("p (a c) -> p a c", c=8)
        k = V(lambda e: e.tensor_reduce(g[:, 320:324], l3, AX.X, ALU.max), k)
        k = V(lambda e: e.tensor_tensor(l3, l3, g[:, 320:324].rearrange("p (a c) -> p a c", c=1)
                                        .to_broadcast([128, 4, 8]), ALU.subtract), k)
        k = A(lambda e: e.activation(lg, lg, ACT.Exp), k)
        k = V(lambda e: e.tensor_tensor(lg, lg, g[:, 288:320], ALU.mult), k)
        k = V(lambda e: e.tensor_reduce(g[:, 320:324], l3, AX.X, ALU.add), k)
        k = V(lambda e: e.reciprocal(g[:, 324:328], g[:, 320:324]), k)
        k = V(lambda e: e.tensor_tensor(l3, l3, g[:, 324:328].rearrange("p (a c) -> p a c", c=1)
                                        .to_broadcast([128, 4, 8]), ALU.mult), k)
        i = pan[0] % 3
        pan[0] += 1
        b2 = PA[i]

        def fn2(e):
            for tb in range(4):
                m = e.transpose(b2[0:8, tb * 128:tb * 128 + 128], g[:, tb * 8:tb * 8 + 8], ident)
            return m
        kt_ = T(fn2, k, pa_free[i])
        kt_ = V(lambda e: e.tensor_copy(t2[0:8, :], b2[0:8, :]), kt_)
        kt_ = T(lambda e: e.matmul(b2[:, :], cst[0:8, C_SEL:C_SEL + 128], t2[0:8, :], start=True, stop=True), kt_)
        kt_ = V(lambda e: e.tensor_scalar(t2[:, :], b2[:, :], 2.0, None, ALU.mult), kt_)
        pa_free[i] = kt_
        order([(wl[:, 4 * c:4 * c + 4, :], 4) for c in range(4)])
        i, bank, kp = project(X, [xk])
        kp = V(lambda e, bank=bank: e.tensor_tensor(t2[:, :], bank[:, :], t2[:, :], ALU.mult), kp, kt_)
        pa_free[i] = kp
        a = A(lambda e: e.activation(lgh[:, :], t2[:, :], ACT.Copy), kp, need)
        return V(lambda e: e.tensor_tensor(lgl[:, :], t2[:, :], lgh[:, :].bitcast(F32), ALU.subtract), a)

    def ffn_half(h, X, xk, need, x2k):
        kl_ = gates(X, xk, need)
        for nb in range(16):
            order(wblock(wb, nb, True))
        for nb in range(16):
            s = rcn[0] % 2
            rcn[0] += 1
            kr_ = Q.D("sync", d_rc[s], rc[s][:, :], x2d[:, h, nb, :], rc_free[s], *x2k)
            i, bank, k = project(X, [xk], (lgh, lgl, kl_))
            k = V(lambda e, s=s, bank=bank, nb=nb: e.scalar_tensor_tensor(
                ev[s][:, :], bank[:, :], bbs[:, nb:nb + 1], rc[s][:, :], ALU.add, ALU.add), k, kr_, ev_free[s])
            pa_free[i] = k
            rc_free[s] = k
            ev_free[s] = Q.D("sync", d_o[s], out[:, h, nb, :], ev[s][:, :], k)
        return k

    Zg = at(qr_off, [544])
    ka = A(lambda e: e.activation(gwh[:, :, :], gwr[:, :, :], ACT.Copy), k_c)
    k_gw = V(lambda e: e.tensor_tensor(gwl[:, :, :], gwr[:, :, :], gwh[:, :, :].bitcast(F32), ALU.subtract), ka)

    XX = (XH_, XL_)
    AX2 = (ATH, ATL)
    k = lnsplit(XF0, AF0[:, :, :], XH_, XL_, [k_sx1])
    kat, kxd = qkv_attention(XX, [k], k_x1[1], k_x1[1])
    kl1 = Q.D("sync", d_ln, XF0[:, :, :], x1d[:, 1, :, :], k_sx1, kxd)
    k1 = lnsplit(XF0, XF1[:, :, :], XH_, XL_, [kl1])
    ks2, kwo = wo_half(0, AX2, kat)
    kat2, kxd2 = qkv_attention(XX, [k1], None, kwo)
    kl2 = Q.D("sync", d_ln, XF0[:, :, :], x2d[:, 0, :, :], *ks2, kxd2)
    k2 = lnsplit(XF0, XF1[:, :, :], XH_, XL_, [kl2])
    ks3, kwo2 = wo_half(1, AX2, kat2)
    kl3 = Q.D("sync", d_ln, AF1[:, :, :], x2d[:, 1, :, :], *ks3, kwo2)
    kf = ffn_half(0, XX, k2, kat2, ks2)
    k3 = lnsplit(AF1, AF0[:, :, :], ATH, ATL, [kl3])
    ffn_half(1, AX2, k3, kf, ks3)
    Q.q["sync"].append((tuple(ev_free), None, None, 0))

    with nc.Block() as block:
        @block.sync
        def _(e):
            Q.emit("sync", e)

        @block.scalar
        def _(e):
            Q.emit("scalar", e)

        @block.gpsimd
        def _(e):
            Q.emit("gpsimd", e)

        @block.vector
        def _(e):
            Q.emit("vector", e)

        @block.tensor
        def _(e):
            Q.emit("tensor", e)
    return Q


def layout(x, ctx_4096, conv_w, gamma, beta, wq, wk, wv, wo, gate_w, base_w, base_b, lora_A, lora_B):
    f = lambda a: np.asarray(a)
    ac = np.ascontiguousarray
    x, ctx = f(x), f(ctx_4096)
    xt = ac(x.reshape(2, HT, 128, NT).transpose(2, 0, 3, 1))
    ctxT = ac(ctx.transpose(0, 2, 1))
    cols = np.array([(4 * (2 * j + s) + r) * 64 + d for j in range(4) for r in range(4) for s in range(2)
                     for d in range(64)])
    w = np.concatenate([f(wq)[:, cols], f(wk), f(wv)], axis=1)
    wqkv = ac(w.reshape(128, NT, 24, 128).transpose(2, 0, 1, 3))
    wo_ = ac(f(wo)[cols, :].reshape(16, 128, 128, NT).transpose(3, 1, 0, 2))
    la = f(lora_A).reshape(128, L).T
    wl = ac(la.reshape(128, NT, 128))
    bw = f(base_w).T.reshape(128, NT, 128, NT).transpose(3, 0, 1, 2)
    lb = f(lora_B).transpose(0, 2, 1).reshape(128, 128, NT).transpose(2, 0, 1)
    wb = ac(np.concatenate([bw, lb[:, :, None, :]], axis=2))
    gw = ac(f(gate_w).T.reshape(128, NT, 8))
    bb = ac(f(base_b).reshape(128, NT))
    cw = ac(np.broadcast_to(f(conv_w).reshape(1, 14), (128, 14)))
    bn = ac(np.broadcast_to(np.concatenate([f(gamma), f(beta)]).reshape(1, 2), (128, 2)))
    return dict(ctxT=ctxT, xT=xt, cw=cw, bn=bn, cst=constants(), wqkv=wqkv, wo=wo_, wl=wl, wb=wb, gw=gw, bb=bb)


def kernel(x, ctx_4096, L0_xattn_conv_w, L0_xattn_bn_gamma, L0_xattn_bn_beta, L0_attn_wq, L0_attn_wk, L0_attn_wv,
           L0_attn_wo, L0_ffn_gate_w, L0_ffn_base_w, L0_ffn_base_b, L0_ffn_lora_A, L0_ffn_lora_B):
    import concourse.bacc as bacc
    from concourse.bass_utils import run_bass_kernel_spmd

    arrays = layout(x, ctx_4096, L0_xattn_conv_w, L0_xattn_bn_gamma, L0_xattn_bn_beta, L0_attn_wq, L0_attn_wk,
                    L0_attn_wv, L0_attn_wo, L0_ffn_gate_w, L0_ffn_base_w, L0_ffn_base_b, L0_ffn_lora_A,
                    L0_ffn_lora_B)
    nc = bacc.Bacc("TRN2", target_bir_lowering=False, num_devices=1)
    args = [nc.dram_tensor(n, list(a.shape), F32, kind="ExternalInput").ap() for n, a in arrays.items()]
    out = nc.dram_tensor("out", [128, 2, NT, HT], F32, kind="ExternalOutput").ap()
    build(nc, *args, out)
    r = run_bass_kernel_spmd(nc, [arrays], core_ids=[0])
    got = r.results[0]["out"]
    return np.ascontiguousarray(got.transpose(1, 3, 0, 2)).reshape(B, C, L)
```

```python
import numpy as np
import concourse.bass as bass
import concourse.mybir as mybir

F32 = mybir.dt.float32
F32R = mybir.dt.float32r
BF16 = mybir.dt.bfloat16
ALU = mybir.AluOpType
ACT = mybir.ActivationFunctionType
AX = mybir.AxisListType

B, C, L, CM = 16, 64, 2048, 1601
K = 38
NT = 16
HT = 512
HB = 8
EPS = 1e-5
FMAX = 3.4028234663852886e38
TINY = 1e-20
U32 = mybir.dt.uint32
NEG = -1.0e30

C_ONES, C_SHL, C_SHR, C_ID, C_MASK, C_COS, C_SIN, C_TRI, C_SEL, C_IOTA, C_END = 0, 128, 256, 384, 512, 576, 640, 704, 768, 896, 960


def constants():
    c = np.zeros((128, C_END), np.float32)
    c[:, C_ONES:C_ONES + 128] = 1.0
    for p in range(128):
        if p >= 1:
            c[p - 1, C_SHL + p] = 1.0
        if p <= 126:
            c[p + 1, C_SHR + p] = 1.0
        c[p, C_ID + p] = 1.0
    q = np.arange(128)
    c[:, C_MASK:C_MASK + 64] = np.where(np.arange(64)[None, :] <= q[:, None] % 64, 0.0, NEG)
    c[:, C_IOTA:C_IOTA + 64] = np.arange(64)[None, :]
    freqs = (np.float32(1.0) / np.float32(10000.0) ** (np.arange(0, 64, 2, dtype=np.float32) / np.float32(64))).astype(np.float32)
    ang = np.outer(np.arange(64, dtype=np.float32), freqs).astype(np.float32)
    d = q % 64
    c[:, C_COS:C_COS + 64] = np.cos(ang)[:, d // 2].T
    c[:, C_SIN:C_SIN + 64] = np.where(d % 2 == 0, -1.0, 1.0)[:, None] * np.sin(ang)[:, d // 2].T
    e = np.arange(8)
    c[:, C_TRI:C_TRI + 64] = (e[None, :] < e[:, None]).astype(np.float32).reshape(1, 64)
    for k in range(8):
        c[k, C_SEL + 16 * k:C_SEL + 16 * k + 16] = 1.0
    return c


def row_numbers():
    p, b, t = np.meshgrid(np.arange(128), np.arange(B), np.arange(NT), indexing="ij")
    return (b * L + p * NT + t + 1).astype(np.float32).reshape(128, B * NT)


class Queues:

    def __init__(self, nc):
        self.nc = nc
        self.q = {n: [] for n in ("vector", "scalar", "gpsimd", "tensor", "sync")}
        self.sem = {n: nc.alloc_semaphore("s_" + n) for n in ("vector", "scalar", "gpsimd", "tensor")}
        self.count = {n: 0 for n in self.sem}
        self.dcount = {}

    def op(self, eng, fn, waits):
        self.count[eng] += 1
        self.q[eng].append((waits, fn, self.sem[eng], 1))
        return (self.sem[eng], self.count[eng])

    def V(self, fn, *w):
        return self.op("vector", fn, w)

    def A(self, fn, *w):
        return self.op("scalar", fn, w)

    def P(self, fn, *w):
        return self.op("gpsimd", fn, w)

    def T(self, fn, *w):
        return self.op("tensor", fn, w)

    def D(self, eng, sem, out, in_, *w):
        self.dcount[sem] = self.dcount.get(sem, 0) + 16
        self.q[eng].append((w, lambda e: e.dma_start(out, in_), sem, 16))
        return (sem, self.dcount[sem])

    def last(self, eng):
        return (self.sem[eng], self.count[eng])

    def emit(self, eng, e):
        seen = {}
        for waits, fn, sem, inc in self.q[eng]:
            for t in waits:
                if t is not None and seen.get(t[0], 0) < t[1]:
                    e.wait_ge(t[0], t[1])
                    seen[t[0]] = t[1]
            if fn is None:
                continue
            fn(e).then_inc(sem, inc)


def build(nc, ctxT, xT, cw, bn, cst_d, rn, wqkv, wo, wl, wb, gw, bb, out):
    Q = Queues(nc)
    V, A, P, T = Q.V, Q.A, Q.P, Q.T
    x1d = nc.dram_tensor("x1d", [128, 2, NT, HT], F32).ap()
    x2d = nc.dram_tensor("x2d", [128, 2, NT, HT], F32).ap()
    base = (nc.sbuf_base + 63) // 64 * 64
    names = [0]

    def at(off, shape, dt=F32):
        names[0] += 1
        return nc.alloc_sbuf_tensor_at(f"t{names[0]}", [128] + shape, dt, offset=base + off)

    KB = 1024
    top = [128 * KB]

    def sb(shape, dt=F32):
        n = 1
        for s in shape:
            n *= s
        n *= 2 if dt == BF16 else 4
        off = top[0]
        top[0] += (n + 31) // 32 * 32
        return at(off, shape, dt)

    def sem(n):
        return nc.alloc_semaphore(n)

    XN = at(0, [2, NT, HT])
    ATH = at(0, [NT, HT], F32R)
    ATL = at(32 * KB, [NT, HT], F32R)
    AF0 = at(0, [NT, HT])
    AF1 = at(32 * KB, [NT, HT])
    XF0 = at(64 * KB, [NT, HT])
    XF1 = at(96 * KB, [NT, HT])
    XL_ = at(64 * KB, [NT, HT], F32R)
    XH_ = at(96 * KB, [NT, HT], F32R)
    AL_ = ATL
    NR = 8
    RS = (CM * 4 + 63) // 64 * 64
    ring = [at(64 * KB + i * RS, [CM]) for i in range(NR)]
    o = 64 * KB + NR * RS
    Mb = []
    for i in range(3):
        Mb.append(at(o, [CM], BF16))
        o += 3232
    scr = at(o, [CM], BF16); o += 3232
    L4 = at(o, [2, NT, 4])
    dq = [at(o + 256 * y, [NT, 7], BF16) for y in range(2)]
    o += 512
    L2 = at(o, [2, NT, 2]); o += 256
    nT = at(o, [2, 2]); o += 32
    assert o <= 128 * KB, o
    G = ring[0]
    pend_ = at(64 * KB + RS + 3 * KB + 256, [1])
    w256 = at(64 * KB + RS, [256])
    oh = at(64 * KB + RS + KB, [256], U32)
    c64 = at(64 * KB + RS + 2 * KB, [64])
    eqb = at(64 * KB + RS + 2 * KB + 256, [64])
    prb = at(64 * KB + RS + 2 * KB + 512, [64])
    tk = at(64 * KB + RS + 2 * KB + 768, [40])
    sm = at(64 * KB + RS + 3 * KB, [16])
    idx = at(64 * KB + RS + 3 * KB + 64, [1], U32)
    fl2 = at(64 * KB + RS + 3 * KB + 128, [4])
    flu = at(64 * KB + RS + 3 * KB + 192, [2], U32)
    ke = at(64 * KB + 2 * RS, [NT, C], U32)
    kf2 = at(64 * KB + 3 * RS, [NT, C])
    crc = [at(64 * KB + i * 4 * KB, [NT, C]) for i in range(2)]
    sbc = [at(72 * KB + i * 4 * KB, [NT, C]) for i in range(2)]
    jnk = at(80 * KB, [C])
    Yp = at(88 * KB, [4 * B, 22])

    mask_off = top[0]
    kT = sb([4, HT])
    Vt = sb([4, HT])
    SB = [sb([HT]) for _ in range(2)]
    PTs = [sb([HT]) for _ in range(2)]
    qr_off = top[0]
    qr = [sb([HT]) for _ in range(2)]
    qs_off = top[0]
    qs = sb([HT])
    t1 = sb([HT])
    raw = [sb([4, 128]) for _ in range(4)]
    wh = [sb([4, 128], F32R) for _ in range(4)]
    wlo = [sb([4, 128], F32R) for _ in range(4)]
    rc = [sb([HT]) for _ in range(2)]
    ev = [sb([HT]) for _ in range(2)]
    assert top[0] - mask_off >= 64 * KB
    cand = at(mask_off, [B, NT, C])
    lsq = [at(mask_off + 60 * KB + 2 * KB * i, [HT]) for i in range(2)]
    gwr = at(mask_off + 56 * KB, [NT, 8])
    cst = sb([C_END])
    Mn = sb([HT])
    Rs = sb([HT])
    r1_off = top[0]
    R1 = sb([HT])
    thr = at(r1_off, [B, NT])
    cut = at(r1_off + KB, [B, NT])
    stat_off = top[0]
    stat = sb([4, B, NT])
    flg = at(stat_off, [B, NT])
    rid = at(stat_off + KB, [B, NT])
    v8 = at(stat_off + 2 * KB, [2, NT, 8])
    cnt = at(stat_off + 3 * KB, [3, 2, NT])
    ins = at(stat_off + 3 * KB + 384, [3, 2, NT], U32)
    identb = at(stat_off + 3 * KB + 768, [128], BF16)
    lgh = at(stat_off, [HT], F32R)
    lgl = at(stat_off + 2 * KB, [HT], F32R)
    t2 = at(qs_off, [HT])
    gwh = sb([NT, 8], F32R)
    gwl = sb([NT, 8], F32R)
    bbs = sb([NT])
    w16 = sb([16])
    sc = sb([160])
    assert top[0] <= nc.sbuf_usable_end - base, top[0]
    Z = at(88 * KB + 4 * B * 22 * 4, [2, 256])
    Zt = at(88 * KB + 4 * B * 22 * 4 + 2048, [2, 256])
    A12 = at(88 * KB + 4 * B * 22 * 4 + 4096, [2, 256])
    Dm = stat[:, 0, :, :]
    A2 = stat[:, 1, :, :]

    ps = [nc.alloc_psum_tensor(f"ps{i}", [128, 512], F32) for i in range(8)]
    PA, PS_, PT, PO = ps[0:3], ps[3], ps[4:6], ps[6:8]

    d_c = sem("d_c"); d_x = [sem("d_x0"), sem("d_x1")]
    d_r = [sem(f"d_r{i}") for i in range(NR)]
    d_w = [sem(f"d_w{i}") for i in range(4)]
    d_xr = [sem("d_xr0"), sem("d_xr1")]
    d_s = sem("d_s"); d_s2 = sem("d_s2"); d_rc = [sem("d_rc0"), sem("d_rc1")]
    d_o = [sem("d_o0"), sem("d_o1")]
    d_ln = sem("d_ln")

    ones = cst[:, C_ONES:C_ONES + 128]
    ident = cst[:, C_ID:C_ID + 128]

    k_c = Q.D("sync", d_c, cst[:, :], cst_d)
    k_c = Q.D("sync", d_c, w16[:, 0:14], cw)
    k_c = Q.D("sync", d_c, w16[:, 14:16], bn)
    k_c = Q.D("sync", d_c, bbs[:, :], bb)
    k_c = Q.D("sync", d_c, gwr[:, :, :], gw)
    k_c = Q.D("sync", d_c, rid[:, :, :], rn.rearrange("p (b t) -> p b t", t=NT))
    k_x = [Q.D("sync", d_x[h], XN[:, h, :, :], xT[:, h, :, :]) for h in range(2)]

    def over_t(ap):
        return ap.rearrange("p t n -> p n t")

    def bc(ap, n):
        return ap.rearrange("p (a n) -> p a n", a=1).to_broadcast([128, n, HT])

    def layernorm(x, scratch, bank, waits, bank_free):
        k = V(lambda e: e.tensor_reduce(R1[:, :], over_t(x[:, :, :]), AX.X, ALU.add), *waits)
        k = T(lambda e: e.matmul(bank[:, :], ones, R1[:, :], start=True, stop=True), k, bank_free, k_c)
        k = V(lambda e: e.tensor_scalar(Mn[:, :], bank[:, :], 1.0 / L, None, ALU.mult), k)
        a = V(lambda e: e.tensor_tensor(x[:, 0:11, :], x[:, 0:11, :], bc(Mn[:, :], 11), ALU.subtract), k)
        b = P(lambda e: e.tensor_tensor(x[:, 11:16, :], x[:, 11:16, :], bc(Mn[:, :], 5), ALU.subtract), k)
        k1 = A(lambda e: e.activation(scratch[:, 0:11, :], x[:, 0:11, :], ACT.Square), a)
        k2 = A(lambda e: e.activation(scratch[:, 11:16, :], x[:, 11:16, :], ACT.Square), b)
        k = V(lambda e: e.tensor_reduce(R1[:, :], over_t(scratch[:, :, :]), AX.X, ALU.add), k1, k2)
        k = T(lambda e: e.matmul(bank[:, :], ones, R1[:, :], start=True, stop=True), k)
        k = V(lambda e: e.tensor_scalar(Mn[:, :], bank[:, :], 1.0 / L, EPS, ALU.mult, ALU.add), k)
        bf = k
        k = A(lambda e: e.activation(R1[:, :], Mn[:, :], ACT.Sqrt), k)
        k = V(lambda e: e.reciprocal(Rs[:, :], R1[:, :]), k)
        return k, bf

    kgh = A(lambda e: e.activation(gwh[:, :, :], gwr[:, :, :], ACT.Copy), k_c)
    k_gw = V(lambda e: e.tensor_tensor(gwl[:, :, :], gwr[:, :, :], gwh[:, :, :].bitcast(F32), ALU.subtract), kgh)
    k_idb = V(lambda e: e.tensor_copy(identb[:, :], ident), k_c)

    def ln0():
        sq = [None, None]
        b0 = None
        for h in range(2):
            x = XN[:, h, :, :]

            def total_of(e, x=x):
                for t in range(NT):
                    m = e.matmul(ps[6][:, :], ones, x[:, t, :], start=(t == 0), stop=(t == NT - 1))
                return m
            k = T(total_of, k_x[h], k_c, b0)
            km = A(lambda e: e.activation(Mn[:, :], ps[6][:, :], ACT.Copy, scale=1.0 / L), k,
                   Q.last("gpsimd") if h else None)
            for t in range(NT):
                xt = x[:, t, :]
                k1 = P(lambda e, xt=xt: e.tensor_tensor(xt, xt, Mn[:, :], ALU.subtract), km)
                k2 = P(lambda e, xt=xt, t=t: e.tensor_tensor(lsq[t % 2][:, :], xt, xt, ALU.mult), k1, sq[t % 2])
                yield
                sq[t % 2] = T(lambda e, t=t: e.matmul(ps[7][:, :], ones, lsq[t % 2][:, :],
                                                      start=(t == 0), stop=(t == NT - 1)), k2, b0 if t == 0 else None)
            k = V(lambda e: e.tensor_scalar(Mn[:, :], ps[7][:, :], 1.0 / L, EPS, ALU.mult, ALU.add), sq[1])
            b0 = k
            k = A(lambda e: e.activation(Mn[:, :], Mn[:, :], ACT.Sqrt), k)
            k = V(lambda e: e.reciprocal(Rs[:, :], Mn[:, :]), k)
            for t in range(NT):
                xt = x[:, t, :]
                P(lambda e, xt=xt: e.tensor_tensor(xt, xt, Rs[:, :], ALU.mult), k)
                if t % 2:
                    yield
        yield

    NG = B * NT // 2
    bankf = [None] * 6
    bankn = [0]
    mbf = [None] * 3
    mbn = [0]
    freed = [[] for _ in range(NR)]
    kl, kA, kB, kC, kD, kv8 = {}, {}, {}, {}, {}, {}
    kcp = {}
    SHRINK = float(np.float32(1.0) - np.float32(2.0 ** -24))
    k_scr = [None]
    k_thr = V(lambda e: e.memset(thr[:, :, :], FMAX))
    k_cut = V(lambda e: e.memset(cut[:, :, :], float(C)))
    small_free = [[], []]

    def where(n):
        return n // NT % 2, n % NT

    def load(n):
        s = n % NR
        b, t = n // NT, n % NT
        kl[n] = Q.D("sync", d_r[s], ring[s][:, :], ctxT[b].rearrange("(p t) c -> p t c", t=NT)[:, t, :], *freed[s])

    def cand_copy(n):
        b, t = n // NT, n % NT
        kcp[n] = P(lambda e, n=n, b=b, t=t: e.tensor_copy(cand[:, b, t, :], ring[n % NR][:, 0:C]), kl[n],
                   k_gw if b >= 14 else None, k_ln0[0] if b == 15 else None)

    def stage_a(g):
        for n in (2 * g, 2 * g + 1):
            y, t = where(n)
            if t == 0:
                for w in small_free[y]:
                    pass
            k = V(lambda e, n=n, y=y, t=t: e.max(v8[:, y, t, :], ring[n % NR][:, 0:C]), kl[n], *small_free[y])
        y, t = where(2 * g)
        k = V(lambda e, y=y, t=t, g=g: e.tensor_scalar(nT[:, g % 2, :], v8[:, y, t:t + 2, 3], TINY, -1.0,
                                                       ALU.max, ALU.mult), k, kA.get(g - 2))
        for n in (2 * g, 2 * g + 1):
            y, t = where(n)
            k_scr[0] = A(lambda e, n=n, y=y, t=t, g=g: e.activation(
                scr[:, :], ring[n % NR][:, :], ACT.Sign, bias=nT[:, g % 2, n % 2:n % 2 + 1], scale=SHRINK,
                accum_out=cnt[:, 0, y, t:t + 1]), k, k_scr[0])
        kA[g] = k_scr[0]

    def count(n, step, sc_ap, kw):
        m = mbn[0] % 3
        mbn[0] += 1
        q = bankn[0] % 6
        bankn[0] += 1
        y, t = where(n)
        k = V(lambda e, m=m, n=n: e.tensor_scalar(Mb[m][:, :], ring[n % NR][:, :], sc_ap, None, ALU.is_gt), kw, mbf[m])
        kc = k

        def fn(e, m=m, q=q):
            for c in range(13):
                w = min(128, CM - 128 * c)
                mm = e.matmul(ps[q][:, 0:w], identb[:, :], Mb[m][:, 128 * c:128 * c + w], start=(c == 0), stop=(c == 12))
            return mm
        k = T(fn, k, bankf[q], k_idb)
        mbf[m] = k
        return q, k, kc, (y, t, step)

    def gather_counts(lst):
        for q, k, _, (y, t, step) in lst:
            k_scr[0] = bankf[q] = A(lambda e, q=q, y=y, t=t, step=step: e.activation(
                scr[:, 0:128], ps[q][:, 0:128], ACT.Copy, accum_out=cnt[:, step, y, t:t + 1]), k, k_scr[0])
        return k_scr[0]

    def narrow(y, t, step, bound, kin, dst, src, half):
        k = V(lambda e: e.tensor_scalar(ins[:, step, y, t:t + 2], cnt[:, step, y, t:t + 2], bound, None, ALU.is_lt), kin)
        V(lambda e: e.tensor_copy(dst, src[:, :, 0:half]))
        k = Q.last("vector")
        w = ins[:, step, y, t:t + 2].rearrange("p (a n) -> p a n", n=1).to_broadcast([128, 2, half])
        return V(lambda e: e.copy_predicated(dst, w, src[:, :, half:2 * half]), k)

    cB, cC = {}, {}

    def stage_b(g):
        y, t = where(2 * g)
        k = narrow(y, t, 0, 2.0 * K - CM - 1.0, kA[g], L4[:, y, t:t + 2, :], v8[:, y, t:t + 2, :], 4)
        cB[g] = [count(n, 1, L4[:, y, n % NT, 1:2], k) for n in (2 * g, 2 * g + 1)]

    def stage_c(g):
        y, t = where(2 * g)
        k = narrow(y, t, 1, float(K), kB[g], L2[:, y, t:t + 2, :], L4[:, y, t:t + 2, :], 2)
        cC[g] = [count(n, 2, L2[:, y, n % NT, 0:1], k) for n in (2 * g, 2 * g + 1)]
        for i, n in enumerate((2 * g, 2 * g + 1)):
            freed[n % NR] = [cC[g][i][2], kcp[n]]

    def stage_d(b):
        y = b % 2
        i1, i2, i3 = (ins[:, s_, y, :] for s_ in range(3))
        v4, f = v8[:, y, :, 3], flg[:, b, :]
        k = V(lambda e: e.tensor_scalar(i3, cnt[:, 2, y, :], float(K), None, ALU.is_lt), kC[(b + 1) * NT // 2 - 1])
        k = V(lambda e: e.copy_predicated(thr[:, b, :], i1, v4), k)
        k = V(lambda e: e.copy_predicated(thr[:, b, :], i2, L4[:, y, :, 1]), k)
        k = V(lambda e: e.copy_predicated(thr[:, b, :], i3, L2[:, y, :, 0]), k)
        r0, r1 = cnt[:, 0, y, :], cnt[:, 1, y, :]
        e7 = dq[y]
        k = V(lambda e: e.tensor_tensor(f, i1, i2, ALU.mult), k)
        k = V(lambda e: e.tensor_tensor(f, f, i3, ALU.mult), k)
        k = V(lambda e: e.scalar_tensor_tensor(r0, v4, TINY, i1, ALU.is_lt, ALU.mult), k)
        k = V(lambda e: e.tensor_tensor(f, f, r0, ALU.max), k)
        k = V(lambda e: e.tensor_scalar(i1, v4.bitcast(U32), 0x7FFFFF, None, ALU.bitwise_and), k)
        k = V(lambda e: e.tensor_scalar(r0, i1, float(0x7FFFFF), None, ALU.is_equal), k)
        k = V(lambda e: e.tensor_tensor(f, f, r0, ALU.max), k)
        k = V(lambda e: e.tensor_tensor(e7[:, :, :], v8[:, y, :, 0:7], v8[:, y, :, 1:8], ALU.is_equal), k)
        k = V(lambda e: e.tensor_reduce(r1, e7[:, :, :], AX.X, ALU.max), k)
        k = V(lambda e: e.tensor_tensor(f, f, r1, ALU.max), k)
        small_free[y] = [k]
        return k

    bg = ln0()
    k_ln0 = [None]
    next_load = 0
    for n in range(NR):
        load(n)
    next_load = NR
    for i in range(NG + 3):
        if i < NG:
            stage_a(i)
            cand_copy(2 * i)
            cand_copy(2 * i + 1)
        for _ in range(2):
            if bg is not None and next(bg, 1) == 1:
                bg = None
                k_ln0[0] = Q.last("gpsimd")
        if 1 <= i <= NG:
            stage_b(i - 1)
        if 2 <= i <= NG + 1:
            stage_c(i - 2)
            for n in (2 * (i - 2), 2 * (i - 2) + 1):
                if n + NR < B * NT:
                    load(n + NR)
        if 1 <= i <= NG:
            kB[i - 1] = gather_counts(cB[i - 1])
        if 2 <= i <= NG + 1:
            kC[i - 2] = gather_counts(cC[i - 2])
        if i >= 3 and (i - 3) % 8 == 7:
            k_d = stage_d((i - 3) // 8)
    k_srch = k_d
    k_scp = Q.last("gpsimd")

    f_s, h_s, g_s, gd_s, w_s = sem("f_s"), sem("h_s"), sem("g_s"), sem("gd_s"), sem("w_s")
    rows = ctxT.rearrange("b l c -> (b l) c")

    def chain(e):
        n = [0]

        def do(ins_):
            n[0] += 1
            ins_.then_inc(w_s, 1)
            e.wait_ge(w_s, n[0])
        return do

    thf, ctf, flf, rif = (x_[:, :, :].rearrange("p b t -> p (b t)") for x_ in (thr, cut, flg, rid))

    def pick(e, do):
        do(e.tensor_reduce(fl2[:, 0:1], flf, AX.X, ALU.max))
        do(e.tensor_tensor(w256[:, :], flf, rif, ALU.mult))
        do(e.tensor_reduce(sm[:, 8:9], w256[:, :], AX.X, ALU.max))
        do(e.tensor_scalar(sm[:, 9:10], sm[:, 8:9], -1.0, 0.0, ALU.add, ALU.max))
        do(e.tensor_copy(idx[:, :], sm[:, 9:10]))
        e.sem_clear(w_s)
        e.sem_inc(f_s, 1)

    def open_rows_v(e):
        do = chain(e)
        do(e.memset(fl2[:, :], 0.0))
        do(e.memset(sm[:, 10:11], -FMAX))
        do(e.memset(sm[:, 11:12], 0.0))
        pick(e, do)

        def head():
            e.wait_ge(h_s, 1)
            e.sem_clear(h_s)
            return e.value_load(flu[0:1, 0:1])
        with e.While(head):
            e.wait_ge(gd_s, 1)
            e.sem_clear(gd_s)
            do = chain(e)
            do(e.tensor_copy(c64[:, :], G[:, 0:C]))
            for r in range(5):
                do(e.max(tk[:, 8 * r:8 * r + 8], G[:, :]))
                if r < 4:
                    do(e.match_replace(G[:, :], tk[:, 8 * r:8 * r + 8], G[:, :], -FMAX))
            T38 = tk[:, K - 1:K]
            do(e.tensor_scalar(w256[:, 0:40], tk[:, :], T38, None, ALU.is_gt, ALU.add, accum_out=sm[:, 0:1]))
            do(e.tensor_scalar(sm[:, 1:2], sm[:, 0:1], -1.0, float(K), ALU.mult, ALU.add))
            do(e.tensor_scalar(eqb[:, :], c64[:, :], T38, None, ALU.is_equal))
            do(e.tensor_tensor_scan(prb[:, :], cst[:, C_ONES:C_ONES + C], eqb[:, :], 0.0, ALU.mult, ALU.add))
            do(e.tensor_scalar(eqb[:, :], prb[:, :], sm[:, 1:2], None, ALU.is_le, ALU.add, accum_out=sm[:, 2:3]))
            do(e.tensor_scalar(sm[:, 3:4], sm[:, 2:3], float(C), None, ALU.is_lt))
            do(e.tensor_tensor(fl2[:, 1:2], fl2[:, 1:2], sm[:, 3:4], ALU.max))
            do(e.tensor_scalar(oh[:, :], rif, sm[:, 8:9], None, ALU.is_equal))
            do(e.copy_predicated(thf, oh[:, :], T38.to_broadcast([128, 256])))
            do(e.copy_predicated(ctf, oh[:, :], sm[:, 2:3].to_broadcast([128, 256])))
            do(e.copy_predicated(flf, oh[:, :], sm[:, 11:12].to_broadcast([128, 256])))
            pick(e, do)
        with e.If(e.value_load(flu[0:1, 1:2])):
            do = chain(e)
            for b in range(B):
                cb = cand[:, b, :, :]
                tb = thr[:, b, :].rearrange("p (t a) -> p t a", a=1).to_broadcast([128, NT, C])
                ub = cut[:, b, :].rearrange("p (t a) -> p t a", a=1).to_broadcast([128, NT, C])
                io = cst[:, C_IOTA:C_IOTA + C].rearrange("p (a c) -> p a c", a=1).to_broadcast([128, NT, C])
                do(e.tensor_tensor(kf2[:, :, :], cb, tb, ALU.is_equal))
                do(e.tensor_tensor(ke[:, :, :], io, ub, ALU.is_ge))
                do(e.tensor_tensor(ke[:, :, :], ke[:, :, :], kf2[:, :, :], ALU.mult))
                do(e.copy_predicated(cb, ke[:, :, :], sm[:, 10:11].rearrange("p (a n) -> p a n", n=1)
                                     .to_broadcast([128, NT, C])))
            e.sem_clear(w_s)
        return e.tensor_copy(sm[:, 12:13], sm[:, 11:12])

    def open_rows_p(e):
        def head():
            e.wait_ge(f_s, 1)
            e.sem_clear(f_s)
            e.partition_all_reduce(fl2[:, 2:4], fl2[:, 0:2], 128, bass.bass_isa.ReduceOp.max).then_inc(g_s, 1)
            e.wait_ge(g_s, 1)
            e.tensor_copy(flu[:, :], fl2[:, 2:4]).then_inc(g_s, 1)
            e.wait_ge(g_s, 2)
            e.sem_clear(g_s)
            e.sem_inc(h_s, 1)
            return e.value_load(flu[0:1, 0:1])
        with e.While(head):
            e.indirect_dma_start(G[:, :], None, rows, bass.IndirectOffsetOnAxis(ap=idx[:, 0:1], axis=0))\
                .then_inc(d_g, 16)
            e.wait_ge(d_g, 16)
            e.dma_reset(range(d_g.num, d_g.num + 1))
            e.sem_clear(d_g)
            e.sem_inc(gd_s, 1)
        return e.memset(pend_[:, :], 0.0)

    d_g = sem("d_g")
    k_open = V(open_rows_v, k_srch, k_scr[0], k_scp, Q.last("tensor"))
    k_pool = P(open_rows_p)

    cb_free = [None, None]
    k_st = []
    for b in range(B):
        y = b % 2
        xb = XN[:, b // HB, :, (b % HB) * C:(b % HB) * C + C]
        cb = cand[:, b, :, :]
        tb = thr[:, b, :].rearrange("p (t a) -> p t a", a=1).to_broadcast([128, NT, C])
        k = V(lambda e, cb=cb, tb=tb: e.tensor_tensor(cb, cb, tb, ALU.is_ge), k_open, k_pool)
        k1 = P(lambda e, xb=xb, cb=cb, y=y: e.tensor_tensor(crc[y][:, :, :], cb, xb, ALU.mult), k, *(cb_free[y] or []))
        k2 = P(lambda e, xb=xb, y=y: e.tensor_tensor(sbc[y][:, :, :], xb, crc[y][:, :, :], ALU.subtract), k1)
        for t in range(NT):
            ka = A(lambda e, b=b, y=y, t=t: e.activation(jnk[:, :], crc[y][:, t, :], ACT.Copy,
                                                         accum_out=stat[:, 2, b, t:t + 1]), k1, k_scr[0])
            k_scr[0] = ka
        k_st.append((b, y, k1, k2, ka))
        if b >= 1 or b == B - 1:
            for (b_, y_, k1_, k2_, ka_) in ([k_st[b - 1]] if b < B - 1 else k_st[b - 1:]):
                V(lambda e, b=b_, y=y_: e.tensor_reduce(stat[:, 0, b, :], crc[y][:, :, :], AX.X, ALU.max), k1_)
                V(lambda e, b=b_, y=y_: e.tensor_reduce(stat[:, 1, b, :], sbc[y][:, :, :], AX.X, ALU.max), k2_)
                k_cs = V(lambda e, b=b_, y=y_: e.tensor_reduce(stat[:, 3, b, :], sbc[y][:, :, :], AX.X, ALU.add), k2_)
                cb_free[y_] = [k_cs, ka_]
    k_cs2 = k_scr[0]

    Y4 = Yp[:, :, :].rearrange("p (f b) t -> p f b t", f=4)
    k = V(lambda e: e.tensor_scalar(stat[:, 2, :, :], stat[:, 2, :, :], 1.0 / C, C / K, ALU.mult, ALU.mult), k_cs, k_cs2)
    k = V(lambda e: e.tensor_scalar(stat[:, 3, :, :], stat[:, 3, :, :], 1.0 / C, C / (C - K), ALU.mult, ALU.mult), k)
    st = stat[:, :, :, :].rearrange("p f b t -> p (f b) t")
    kk = V(lambda e: e.tensor_copy(Yp[:, :, 3:19], st), k)
    kl = T(lambda e: e.matmul(PA[1][:, 0:192].rearrange("p (g t) -> p g t", t=3), cst[:, C_SHL:C_SHL + 128],
                              st[:, :, 13:16], start=True, stop=True), k)
    kr = T(lambda e: e.matmul(PA[2][:, 0:192].rearrange("p (g t) -> p g t", t=3), cst[:, C_SHR:C_SHR + 128],
                              st[:, :, 0:3], start=True, stop=True), k)
    kl = V(lambda e: e.tensor_copy(Yp[:, :, 0:3], PA[1][:, 0:192].rearrange("p (g t) -> p g t", t=3)), kl)
    k = V(lambda e: e.tensor_copy(Yp[:, :, 19:22], PA[2][:, 0:192].rearrange("p (g t) -> p g t", t=3)), kr)
    Zf = Z[:, :, :].rearrange("p s (b t) -> p (s b) t", t=NT)
    for ch in range(2):
        for tap in range(7):
            src = Yp[:, ch * 32:ch * 32 + 32, tap:tap + 16]
            wsc = w16[:, ch * 7 + tap:ch * 7 + tap + 1]
            if ch == 0 and tap == 0:
                k = V(lambda e, src=src, wsc=wsc: e.tensor_scalar(Zf, src, wsc, None, ALU.mult), k, k_c)
            else:
                k = V(lambda e, src=src, wsc=wsc: e.scalar_tensor_tensor(Zf, src, wsc, Zf, ALU.mult, ALU.add), k)

    def total(src, col):
        k1 = V(lambda e: e.tensor_reduce(sc[:, col + 2:col + 4], src, AX.X, ALU.add), k)
        k2 = T(lambda e: e.matmul(PA[1][:, 0:2], ones, sc[:, col + 2:col + 4], start=True, stop=True), k1)
        return V(lambda e: e.tensor_scalar(sc[:, col:col + 2], PA[1][:, 0:2], 1.0 / (B * L), None, ALU.mult), k2)

    k = total(Z[:, :, :], 0)
    for s in range(2):
        k = V(lambda e, s=s: e.tensor_scalar(Z[:, s, :], Z[:, s, :], sc[:, s:s + 1], None, ALU.subtract), k)
    k = V(lambda e: e.tensor_tensor(Zt[:, :, :], Z[:, :, :], Z[:, :, :], ALU.mult), k)
    k = total(Zt[:, :, :], 4)
    k = V(lambda e: e.tensor_scalar(sc[:, 8:10], sc[:, 4:6], EPS, None, ALU.add), k)
    k = A(lambda e: e.activation(sc[:, 10:12], sc[:, 8:10], ACT.Sqrt), k)
    k = V(lambda e: e.reciprocal(sc[:, 12:14], sc[:, 10:12]), k)
    for s in range(2):
        k = V(lambda e, s=s: e.tensor_scalar(Z[:, s, :], Z[:, s, :], sc[:, 12 + s:13 + s], w16[:, 14:15],
                                             ALU.mult, ALU.mult), k)
    k = V(lambda e: e.tensor_scalar(Z[:, :, :], Z[:, :, :], w16[:, 15:16], 0.0, ALU.add, ALU.max), k)
    k = A(lambda e: e.activation(Zt[:, :, :], Z[:, :, :], ACT.Exp, scale=-1.0), k)
    k = V(lambda e: e.tensor_scalar(Zt[:, :, :], Zt[:, :, :], 1.0, None, ALU.add), k)
    k = V(lambda e: e.reciprocal(A12[:, :, :], Zt[:, :, :]), k)
    k = V(lambda e: e.tensor_tensor(Dm, A12[:, 0, :].rearrange("p (b t) -> p b t", t=NT),
                                    A12[:, 1, :].rearrange("p (b t) -> p b t", t=NT), ALU.subtract), k)
    k_g = V(lambda e: e.tensor_copy(A2, A12[:, 1, :].rearrange("p (b t) -> p b t", t=NT)), k)

    k_xr = [Q.D("sync", d_xr[h], (XF0, XF1)[h][:, :, :], xT[:, h, :, :], k_g) for h in range(2)]
    k_x1 = []
    adds = []
    for b in range(B):
        h = b // HB
        xr = (XF0, XF1)[h][:, :, (b % HB) * C:(b % HB) * C + C]
        xb = XN[:, h, :, (b % HB) * C:(b % HB) * C + C]
        dm = Dm[:, b, :].rearrange("p (t a) -> p t a", a=1).to_broadcast([128, NT, C])
        a2 = A2[:, b, :].rearrange("p (t a) -> p t a", a=1).to_broadcast([128, NT, C])
        u = cand[:, b, :, :]
        k = V(lambda e, u=u, dm=dm: e.tensor_tensor(u, u, dm, ALU.mult), k_g)
        k = V(lambda e, u=u, a2=a2: e.tensor_tensor(u, u, a2, ALU.add), k)
        k = P(lambda e, u=u, xb=xb: e.tensor_tensor(u, u, xb, ALU.mult), k)
        adds.append((u, xr, k, h))
        if b > 0 or b == B - 1:
            for lu, lx, lk, lh in adds[:len(adds) if b % HB == HB - 1 else -1]:
                kx = V(lambda e, lu=lu, lx=lx: e.tensor_tensor(lx, lx, lu, ALU.add), lk, k_xr[lh])
            adds = adds[len(adds):] if b % HB == HB - 1 else adds[-1:]
        if b % HB == HB - 1:
            k_x1.append(kx)
    k_sx1 = [Q.D("sync", d_s, x1d[:, h, :, :], (XF0, XF1)[h][:, :, :], k_x1[h]) for h in range(2)]
    k_sx1 = k_sx1[1]

    NH_ = len(wh)
    wst = {"n": 0, "raw": [k_x1[1]] * 4, "wf": [k_x1[1]] * NH_}

    def chunk(src, nk):
        n = wst["n"]
        wst["n"] += 1
        r, s = n % 4, n % NH_
        k = Q.D("sync", d_w[r], raw[r][:, 0:nk, :], src, wst["raw"][r])
        rr, hh, ll = raw[r][:, 0:nk, :], wh[s][:, 0:nk, :], wlo[s][:, 0:nk, :]
        k = A(lambda e: e.activation(hh, rr, ACT.Copy), k, wst["wf"][s])
        k = P(lambda e: e.tensor_tensor(ll, rr, hh.bitcast(F32), ALU.subtract), k, wst["wf"][s])
        wst["raw"][r] = k
        return s, k

    pend = []

    def order(items):
        for it in items:
            pend.append(it)

    AHEAD = 2
    ready = []

    def feed():
        while pend and len(ready) < AHEAD + 1:
            ready.append(chunk(*pend.pop(0)))

    pa_free = [None] * 3
    pan = [0]

    def project(X, xk, extra=None):
        i = pan[0] % 3
        pan[0] += 1
        bank = PA[i]
        XHx, XLx = X
        total_ = 4 + (1 if extra else 0)
        for c in range(total_):
            feed()
            s, kw = ready.pop(0)
            nk = 4 if c < 4 else 1

            def fn(e, c=c, s=s, nk=nk):
                for q in range(nk):
                    kt = 4 * c + q
                    xh, xl = (XHx[:, kt, :], XLx[:, kt, :]) if c < 4 else (extra[0][:, :], extra[1][:, :])
                    e.matmul(bank[:, :], wh[s][:, q, :], xl, start=(c == 0 and q == 0), stop=False)
                    e.matmul(bank[:, :], wlo[s][:, q, :], xh, start=False, stop=False)
                    m = e.matmul(bank[:, :], wh[s][:, q, :], xh, start=False, stop=(c == total_ - 1 and q == nk - 1))
                return m
            k = T(fn, kw, *(xk if c == 0 else []), pa_free[i] if c == 0 else None, extra[2] if c == 4 else None)
            wst["wf"][s] = k
        return i, bank, k

    def wblock(w, nb, extra=False):
        src = w[nb]
        out_ = [(src[:, 4 * c:4 * c + 4, :], 4) for c in range(4)]
        if extra:
            out_.append((src[:, 16:17, :], 1))
        return out_

    def lnsplit(x, scratch, hi, lo_, waits):
        i = pan[0] % 3
        pan[0] += 1
        k, bf_ = layernorm(x, scratch, PA[i], waits, pa_free[i])
        pa_free[i] = bf_
        a = V(lambda e: e.tensor_tensor(x[:, 0:11, :], x[:, 0:11, :], bc(Rs[:, :], 11), ALU.mult), k)
        b_ = P(lambda e: e.tensor_tensor(x[:, 11:16, :], x[:, 11:16, :], bc(Rs[:, :], 5), ALU.mult), k)
        a1 = A(lambda e: e.activation(hi[:, 0:8, :], x[:, 0:8, :], ACT.Copy), a)
        a2_ = A(lambda e: e.activation(hi[:, 8:16, :], x[:, 8:16, :], ACT.Copy), a, b_)
        V(lambda e: e.tensor_tensor(lo_[:, 0:8, :], x[:, 0:8, :], hi[:, 0:8, :].bitcast(F32), ALU.subtract), a1)
        return V(lambda e: e.tensor_tensor(lo_[:, 8:16, :], x[:, 8:16, :], hi[:, 8:16, :].bitcast(F32), ALU.subtract), a2_)

    maskc = cst[:, C_MASK:C_MASK + 64].rearrange("p (a n) -> p a n", a=1).to_broadcast([128, 8, 64])
    swap = [i ^ 1 for i in range(32)]

    def rope(dst, bank, k, dst_free):
        cosb = cst[:, C_COS:C_COS + 64].rearrange("p (a n) -> p a n", a=1).to_broadcast([128, 8, 64])
        sinb = cst[:, C_SIN:C_SIN + 64].rearrange("p (a n) -> p a n", a=1).to_broadcast([128, 8, 64])

        def v3(ap):
            return ap.rearrange("p (a n) -> p a n", n=64)
        a = V(lambda e: e.stream_shuffle(qs[:, :], bank[:, :], swap), k, rope_free[0])
        b_ = V(lambda e: e.tensor_tensor(v3(t1[:, :]), v3(bank[:, :]), cosb, ALU.mult), k, rope_free[0])
        c = P(lambda e: e.tensor_tensor(v3(qs[:, :]), v3(qs[:, :]), sinb, ALU.mult), a)
        d = P(lambda e: e.tensor_tensor(dst, t1[:, :], qs[:, :], ALU.add), b_, c, dst_free)
        rope_free[0] = d
        return d, b_

    rope_free = [None]
    st_ = {"S": None, "PT": [None] * 2, "O": None, "SB": [None] * 2, "PTs": [None] * 2, "qr": [None] * 2}

    def qk_scores(i, kq, kk_):
        j, s = i // 4, i % 2

        def fn(e):
            for bb_ in range(HB):
                for hf in range(2):
                    r = slice(64 * hf, 64 * hf + 64)
                    c = slice(64 * bb_, 64 * bb_ + 64)
                    m = e.matmul(PS_[r, c], qr[s][r, c], kT[r, j, c], start=True, stop=True)
            return m
        k = T(fn, kq, kk_, st_["S"])
        st_["qr"][s] = k
        p3 = SB[s][:, :].rearrange("p (a n) -> p a n", n=64)
        s3 = PS_[:, :].rearrange("p (a n) -> p a n", n=64)
        b0 = 16 + s * 32
        k = V(lambda e: e.scalar_tensor_tensor(p3, s3, 0.125, maskc, ALU.mult, ALU.add), k, st_["SB"][s])
        st_["S"] = k
        k = V(lambda e: e.tensor_reduce(sc[:, b0:b0 + 8], p3, AX.X, ALU.max), k)
        mx = sc[:, b0:b0 + 8].rearrange("p (a n) -> p a n", n=1).to_broadcast([128, 8, 64])
        k = V(lambda e: e.tensor_tensor(p3, p3, mx, ALU.subtract), k)
        k = A(lambda e: e.activation(SB[s][:, :], SB[s][:, :], ACT.Exp), k)
        k = V(lambda e: e.tensor_reduce(sc[:, b0 + 8:b0 + 16], p3, AX.X, ALU.add), k)
        k = V(lambda e: e.reciprocal(sc[:, b0 + 16:b0 + 24], sc[:, b0 + 8:b0 + 16]), k)
        rr = sc[:, b0 + 16:b0 + 24].rearrange("p (a n) -> p a n", n=1).to_broadcast([128, 8, 64])
        return V(lambda e: e.tensor_tensor(p3, p3, rr, ALU.mult), k)

    def transpose_p(i, tok):
        s = i % 2

        def fn(e):
            for pr in range(4):
                m = e.transpose(PT[s][:, pr * 128:pr * 128 + 128], SB[s][:, pr * 128:pr * 128 + 128], ident)
            return m
        k = T(fn, tok, st_["PT"][s])
        st_["SB"][s] = k
        k = A(lambda e: e.activation(PTs[s][:, :], PT[s][:, :], ACT.Copy), k, st_["PTs"][s])
        st_["PT"][s] = k
        return k

    def times_v(i, tok, kv, at_free):
        j, s = i // 4, i % 2

        def fn(e):
            for bb_ in range(HB):
                pr, r = bb_ // 2, slice(64 * (bb_ % 2), 64 * (bb_ % 2) + 64)
                for hf in range(2):
                    m = e.matmul(PO[bb_ % 2][64 * hf:64 * hf + 64, 64 * pr:64 * pr + 64],
                                 Vt[r, pr, (2 * j + hf) * 64:(2 * j + hf) * 64 + 64],
                                 PTs[s][r, pr * 128 + 64 * hf:pr * 128 + 64 * hf + 64], start=True, stop=True)
            return m
        k = T(fn, tok, kv, st_["O"])
        st_["PTs"][s] = k
        for z in range(2):
            hi = ATH[:, i, :].rearrange("p (a z n) -> p z a n", z=2, n=64)[:, z]
            lo_ = ATL[:, i, :].rearrange("p (a z n) -> p z a n", z=2, n=64)[:, z]
            src = PO[z][:, 0:256].rearrange("p (a n) -> p a n", n=64)
            a = A(lambda e, hi=hi, src=src: e.activation(hi, src, ACT.Copy), k, at_free)
            b_ = V(lambda e, hi=hi, lo_=lo_, src=src: e.tensor_tensor(lo_, src, hi.bitcast(F32), ALU.subtract), a)
        st_["O"] = b_
        return b_

    def qkv_attention(X, xk, region_free, at_free):
        for nb in range(4):
            order(wblock(wqkv, 16 + nb))
        for nb in range(4):
            order(wblock(wqkv, 20 + nb))
        for nb in range(16):
            order(wblock(wqkv, nb))
        kks = []
        for j in range(4):
            i, bank, k = project(X, xk)
            kd, bf_ = rope(kT[:, j, :], bank, k, region_free)
            pa_free[i] = bf_
            kks.append(kd)
        kvs = []
        vt = None

        def vturn(j, kx):
            def fn(e):
                for tb in range(4):
                    m = e.transpose(PT[j % 2][:, tb * 128:tb * 128 + 128], SB[j % 2][:, tb * 128:tb * 128 + 128], ident)
                return m
            k = T(fn, kx, st_["PT"][j % 2])
            st_["SB"][j % 2] = k
            k = V(lambda e: e.tensor_copy(Vt[:, :, j * 128:j * 128 + 128],
                                          PT[j % 2][:, :].rearrange("p (a n) -> p a n", n=128)), k, region_free)
            st_["PT"][j % 2] = k
            kvs.append(k)
        for j in range(4):
            i, bank, k = project(X, xk)
            kx = V(lambda e, j=j, bank=bank: e.tensor_copy(SB[j % 2][:, :], bank[:, :]), k, st_["SB"][j % 2], region_free)
            pa_free[i] = kx
            if vt:
                vturn(*vt)
            vt = (j, kx)
        sco = {}
        last = None
        for i in range(18):
            if i >= 2:
                pt = transpose_p(i - 2, sco.pop(i - 2))
            if i < 16:
                pi, bank, k = project(X, xk)
                if i == 15:
                    k_x_done = k
                if i == 0:
                    vturn(*vt)
                kq, bf_ = rope(qr[i % 2][:, :], bank, k, st_["qr"][i % 2] or region_free)
                pa_free[pi] = bf_
                kqs = kq if i == 0 else kq
            if i >= 2:
                last = times_v(i - 2, pt, kvs[-1], at_free)
            if i >= 1 and i <= 16:
                sco[i - 1] = qk_scores(i - 1, kprev, kks[-1])
            kprev = kq
        return last, k_x_done

    rcn = [0]
    rc_free = [k_x1[1]] * 2
    ev_free = [k_x1[1]] * 2

    def wo_half(h, X, xk):
        for nb in range(16):
            order(wblock(wo, nb))
        kst = None
        for nb in range(16):
            s = rcn[0] % 2
            rcn[0] += 1
            kr_ = Q.D("sync", d_rc[s], rc[s][:, :], x1d[:, h, nb, :], rc_free[s], k_sx1)
            i, bank, k = project(X, [xk])
            k = V(lambda e, s=s, bank=bank: e.tensor_tensor(ev[s][:, :], bank[:, :], rc[s][:, :], ALU.add), k, kr_, ev_free[s])
            pa_free[i] = k
            rc_free[s] = k
            ev_free[s] = Q.D("sync", d_o[s], x2d[:, h, nb, :], ev[s][:, :], k)
        return list(ev_free), k

    trib = cst[:, C_TRI:C_TRI + 64].rearrange("p (c j) -> p c j", j=8)

    def gates(X, xk, need):
        XHx, XLx = X
        g = Zg
        i = pan[0] % 3
        pan[0] += 1
        b1 = PA[i]

        def fn(e):
            for tb in range(4):
                for kt in range(16):
                    xh = XHx[:, kt, tb * 128:tb * 128 + 128]
                    xl = XLx[:, kt, tb * 128:tb * 128 + 128]
                    o_ = b1[:, tb * 8:tb * 8 + 8]
                    e.matmul(o_, xl, gwh[:, kt, :], start=(kt == 0), stop=False)
                    e.matmul(o_, xh, gwl[:, kt, :], start=False, stop=False)
                    m = e.matmul(o_, xh, gwh[:, kt, :], start=False, stop=(kt == 15))
            return m
        k = T(fn, xk, k_gw, pa_free[i])
        lg = g[:, 0:32]
        k = V(lambda e: e.tensor_copy(lg, b1[:, 0:32]), k, need)
        pa_free[i] = k
        G4 = g[:, 32:288].rearrange("p (a c j) -> p a c j", c=8, j=8)
        H4 = g[:, 288:544].rearrange("p (a c j) -> p a c j", c=8, j=8)
        for tb in range(4):
            lj = g[:, tb * 8:tb * 8 + 8].rearrange("p (a j) -> p a j", a=1).to_broadcast([128, 8, 8])
            lc = g[:, tb * 8:tb * 8 + 8].rearrange("p (c a) -> p c a", a=1).to_broadcast([128, 8, 8])
            k = V(lambda e, tb=tb, lj=lj, lc=lc: e.tensor_tensor(G4[:, tb, :, :], lj, lc, ALU.is_gt), k)
            k = V(lambda e, tb=tb, lj=lj, lc=lc: e.tensor_tensor(H4[:, tb, :, :], lj, lc, ALU.is_equal), k)
            k = V(lambda e, tb=tb: e.tensor_tensor(H4[:, tb, :, :], H4[:, tb, :, :], trib, ALU.mult), k)
        k = V(lambda e: e.tensor_tensor(g[:, 32:288], g[:, 32:288], g[:, 288:544], ALU.add), k)
        k = V(lambda e: e.tensor_reduce(g[:, 288:320], G4.rearrange("p a c j -> p (a c) j"), AX.X, ALU.add), k)
        k = V(lambda e: e.tensor_scalar(g[:, 288:320], g[:, 288:320], 2.0, None, ALU.is_lt), k)
        l3 = lg.rearrange("p (a c) -> p a c", c=8)
        k = V(lambda e: e.tensor_reduce(g[:, 320:324], l3, AX.X, ALU.max), k)
        k = V(lambda e: e.tensor_tensor(l3, l3, g[:, 320:324].rearrange("p (a c) -> p a c", c=1)
                                        .to_broadcast([128, 4, 8]), ALU.subtract), k)
        k = A(lambda e: e.activation(lg, lg, ACT.Exp), k)
        k = V(lambda e: e.tensor_tensor(lg, lg, g[:, 288:320], ALU.mult), k)
        k = V(lambda e: e.tensor_reduce(g[:, 320:324], l3, AX.X, ALU.add), k)
        k = V(lambda e: e.reciprocal(g[:, 324:328], g[:, 320:324]), k)
        k = V(lambda e: e.tensor_tensor(l3, l3, g[:, 324:328].rearrange("p (a c) -> p a c", c=1)
                                        .to_broadcast([128, 4, 8]), ALU.mult), k)
        i = pan[0] % 3
        pan[0] += 1
        b2 = PA[i]

        def fn2(e):
            for tb in range(4):
                m = e.transpose(b2[0:8, tb * 128:tb * 128 + 128], g[:, tb * 8:tb * 8 + 8], ident)
            return m
        kt_ = T(fn2, k, pa_free[i])
        kt_ = V(lambda e: e.tensor_copy(t2[0:8, :], b2[0:8, :]), kt_)
        kt_ = T(lambda e: e.matmul(b2[:, :], cst[0:8, C_SEL:C_SEL + 128], t2[0:8, :], start=True, stop=True), kt_)
        kt_ = V(lambda e: e.tensor_scalar(t2[:, :], b2[:, :], 2.0, None, ALU.mult), kt_)
        pa_free[i] = kt_
        order([(wl[:, 4 * c:4 * c + 4, :], 4) for c in range(4)])
        i, bank, kp = project(X, [xk])
        kp = V(lambda e, bank=bank: e.tensor_tensor(t2[:, :], bank[:, :], t2[:, :], ALU.mult), kp, kt_)
        pa_free[i] = kp
        a = A(lambda e: e.activation(lgh[:, :], t2[:, :], ACT.Copy), kp, need)
        return V(lambda e: e.tensor_tensor(lgl[:, :], t2[:, :], lgh[:, :].bitcast(F32), ALU.subtract), a)

    def ffn_half(h, X, xk, need, x2k):
        kl_ = gates(X, xk, need)
        for nb in range(16):
            order(wblock(wb, nb, True))
        for nb in range(16):
            s = rcn[0] % 2
            rcn[0] += 1
            kr_ = Q.D("sync", d_rc[s], rc[s][:, :], x2d[:, h, nb, :], rc_free[s], *x2k)
            i, bank, k = project(X, [xk], (lgh, lgl, kl_))
            k = V(lambda e, s=s, bank=bank, nb=nb: e.scalar_tensor_tensor(
                ev[s][:, :], bank[:, :], bbs[:, nb:nb + 1], rc[s][:, :], ALU.add, ALU.add), k, kr_, ev_free[s])
            pa_free[i] = k
            rc_free[s] = k
            ev_free[s] = Q.D("sync", d_o[s], out[:, h, nb, :], ev[s][:, :], k)
        return k

    Zg = at(qr_off, [544])

    XX = (XH_, XL_)
    AX2 = (ATH, ATL)
    k = lnsplit(XF0, AF0[:, :, :], XH_, XL_, [k_sx1])
    kat, kxd = qkv_attention(XX, [k], k_x1[1], k_x1[1])
    kl1 = Q.D("sync", d_ln, XF0[:, :, :], x1d[:, 1, :, :], k_sx1, kxd)
    k1 = lnsplit(XF0, XF1[:, :, :], XH_, XL_, [kl1])
    ks2, kwo = wo_half(0, AX2, kat)
    kat2, kxd2 = qkv_attention(XX, [k1], None, kwo)
    kl2 = Q.D("sync", d_ln, XF0[:, :, :], x2d[:, 0, :, :], *ks2, kxd2)
    k2 = lnsplit(XF0, XF1[:, :, :], XH_, XL_, [kl2])
    ks3, kwo2 = wo_half(1, AX2, kat2)
    kl3 = Q.D("sync", d_ln, AF1[:, :, :], x2d[:, 1, :, :], *ks3, kwo2)
    kf = ffn_half(0, XX, k2, kat2, ks2)
    k3 = lnsplit(AF1, AF0[:, :, :], ATH, ATL, [kl3])
    ffn_half(1, AX2, k3, kf, ks3)
    Q.q["sync"].append((tuple(ev_free), None, None, 0))

    with nc.Block() as block:
        @block.sync
        def _(e):
            Q.emit("sync", e)

        @block.scalar
        def _(e):
            Q.emit("scalar", e)

        @block.gpsimd
        def _(e):
            Q.emit("gpsimd", e)

        @block.vector
        def _(e):
            Q.emit("vector", e)

        @block.tensor
        def _(e):
            Q.emit("tensor", e)
    return Q


def layout(x, ctx_4096, conv_w, gamma, beta, wq, wk, wv, wo, gate_w, base_w, base_b, lora_A, lora_B):
    f = lambda a: np.asarray(a)
    ac = np.ascontiguousarray
    x, ctx = f(x), f(ctx_4096)
    xt = ac(x.reshape(2, HT, 128, NT).transpose(2, 0, 3, 1))
    ctxT = ac(ctx.transpose(0, 2, 1))
    cols = np.array([(4 * (2 * j + s) + r) * 64 + d for j in range(4) for r in range(4) for s in range(2)
                     for d in range(64)])
    w = np.concatenate([f(wq)[:, cols], f(wk), f(wv)], axis=1)
    wqkv = ac(w.reshape(128, NT, 24, 128).transpose(2, 0, 1, 3))
    wo_ = ac(f(wo)[cols, :].reshape(16, 128, 128, NT).transpose(3, 1, 0, 2))
    la = f(lora_A).reshape(128, L).T
    wl = ac(la.reshape(128, NT, 128))
    bw = f(base_w).T.reshape(128, NT, 128, NT).transpose(3, 0, 1, 2)
    lb = f(lora_B).transpose(0, 2, 1).reshape(128, 128, NT).transpose(2, 0, 1)
    wb = ac(np.concatenate([bw, lb[:, :, None, :]], axis=2))
    gw = ac(f(gate_w).T.reshape(128, NT, 8))
    bb = ac(f(base_b).reshape(128, NT))
    cw = ac(np.broadcast_to(f(conv_w).reshape(1, 14), (128, 14)))
    bn = ac(np.broadcast_to(np.concatenate([f(gamma), f(beta)]).reshape(1, 2), (128, 2)))
    return dict(ctxT=ctxT, xT=xt, cw=cw, bn=bn, cst=constants(), rn=row_numbers(), wqkv=wqkv, wo=wo_, wl=wl, wb=wb, gw=gw, bb=bb)


def kernel(x, ctx_4096, L0_xattn_conv_w, L0_xattn_bn_gamma, L0_xattn_bn_beta, L0_attn_wq, L0_attn_wk, L0_attn_wv,
           L0_attn_wo, L0_ffn_gate_w, L0_ffn_base_w, L0_ffn_base_b, L0_ffn_lora_A, L0_ffn_lora_B):
    import concourse.bacc as bacc
    from concourse.bass_utils import run_bass_kernel_spmd

    arrays = layout(x, ctx_4096, L0_xattn_conv_w, L0_xattn_bn_gamma, L0_xattn_bn_beta, L0_attn_wq, L0_attn_wk,
                    L0_attn_wv, L0_attn_wo, L0_ffn_gate_w, L0_ffn_base_w, L0_ffn_base_b, L0_ffn_lora_A,
                    L0_ffn_lora_B)
    nc = bacc.Bacc("TRN2", target_bir_lowering=False, num_devices=1)
    args = [nc.dram_tensor(n, list(a.shape), F32, kind="ExternalInput").ap() for n, a in arrays.items()]
    out = nc.dram_tensor("out", [128, 2, NT, HT], F32, kind="ExternalOutput").ap()
    build(nc, *args, out)
    r = run_bass_kernel_spmd(nc, [arrays], core_ids=[0])
    got = r.results[0]["out"]
    return np.ascontiguousarray(got.transpose(1, 3, 0, 2)).reshape(B, C, L)
```

```python
import numpy as np
import concourse.bass as bass
import concourse.mybir as mybir

F32 = mybir.dt.float32
F32R = mybir.dt.float32r
BF16 = mybir.dt.bfloat16
ALU = mybir.AluOpType
ACT = mybir.ActivationFunctionType
AX = mybir.AxisListType

B, C, L, CM = 16, 64, 2048, 1601
K = 38
NT = 16
HT = 512
HB = 8
EPS = 1e-5
FMAX = 3.4028234663852886e38
TINY = 1e-20
U32 = mybir.dt.uint32
NEG = -1.0e30

C_ONES, C_SHL, C_SHR, C_ID, C_MASK, C_COS, C_SIN, C_TRI, C_SEL, C_IOTA, C_END = 0, 128, 256, 384, 512, 576, 640, 704, 768, 896, 960


def constants():
    c = np.zeros((128, C_END), np.float32)
    c[:, C_ONES:C_ONES + 128] = 1.0
    for p in range(128):
        if p >= 1:
            c[p - 1, C_SHL + p] = 1.0
        if p <= 126:
            c[p + 1, C_SHR + p] = 1.0
        c[p, C_ID + p] = 1.0
    q = np.arange(128)
    c[:, C_MASK:C_MASK + 64] = np.where(np.arange(64)[None, :] <= q[:, None] % 64, 0.0, NEG)
    c[:, C_IOTA:C_IOTA + 64] = np.arange(64)[None, :]
    freqs = (np.float32(1.0) / np.float32(10000.0) ** (np.arange(0, 64, 2, dtype=np.float32) / np.float32(64))).astype(np.float32)
    ang = np.outer(np.arange(64, dtype=np.float32), freqs).astype(np.float32)
    d = q % 64
    c[:, C_COS:C_COS + 64] = np.cos(ang)[:, d // 2].T
    c[:, C_SIN:C_SIN + 64] = np.where(d % 2 == 0, -1.0, 1.0)[:, None] * np.sin(ang)[:, d // 2].T
    e = np.arange(8)
    c[:, C_TRI:C_TRI + 64] = (e[None, :] < e[:, None]).astype(np.float32).reshape(1, 64)
    for k in range(8):
        c[k, C_SEL + 16 * k:C_SEL + 16 * k + 16] = 1.0
    return c


def row_numbers():
    p, b, t = np.meshgrid(np.arange(128), np.arange(B), np.arange(NT), indexing="ij")
    return (b * L + p * NT + t + 1).astype(np.float32).reshape(128, B * NT)


class Queues:

    def __init__(self, nc):
        self.nc = nc
        self.q = {n: [] for n in ("vector", "scalar", "gpsimd", "tensor", "sync")}
        self.sem = {n: nc.alloc_semaphore("s_" + n) for n in ("vector", "scalar", "gpsimd", "tensor")}
        self.count = {n: 0 for n in self.sem}
        self.dcount = {}

    def op(self, eng, fn, waits):
        self.count[eng] += 1
        self.q[eng].append((waits, fn, self.sem[eng], 1))
        return (self.sem[eng], self.count[eng])

    def V(self, fn, *w):
        return self.op("vector", fn, w)

    def A(self, fn, *w):
        return self.op("scalar", fn, w)

    def P(self, fn, *w):
        return self.op("gpsimd", fn, w)

    def T(self, fn, *w):
        return self.op("tensor", fn, w)

    def D(self, eng, sem, out, in_, *w):
        self.dcount[sem] = self.dcount.get(sem, 0) + 16
        self.q[eng].append((w, lambda e: e.dma_start(out, in_), sem, 16))
        return (sem, self.dcount[sem])

    def last(self, eng):
        return (self.sem[eng], self.count[eng])

    def emit(self, eng, e):
        seen = {}
        for waits, fn, sem, inc in self.q[eng]:
            for t in waits:
                if t is not None and seen.get(t[0], 0) < t[1]:
                    e.wait_ge(t[0], t[1])
                    seen[t[0]] = t[1]
            if fn is None:
                continue
            fn(e).then_inc(sem, inc)


def build(nc, ctxT, xT, cw, bn, cst_d, rn, wqkv, wo, wl, wb, gw, bb, out):
    Q = Queues(nc)
    V, A, P, T = Q.V, Q.A, Q.P, Q.T
    x1d = nc.dram_tensor("x1d", [128, 2, NT, HT], F32).ap()
    x2d = nc.dram_tensor("x2d", [128, 2, NT, HT], F32).ap()
    base = (nc.sbuf_base + 63) // 64 * 64
    names = [0]

    def at(off, shape, dt=F32):
        names[0] += 1
        return nc.alloc_sbuf_tensor_at(f"t{names[0]}", [128] + shape, dt, offset=base + off)

    KB = 1024
    top = [128 * KB]

    def sb(shape, dt=F32):
        n = 1
        for s in shape:
            n *= s
        n *= 2 if dt == BF16 else 4
        off = top[0]
        top[0] += (n + 31) // 32 * 32
        return at(off, shape, dt)

    def sem(n):
        return nc.alloc_semaphore(n)

    XN = at(0, [2, NT, HT])
    ATH = at(0, [NT, HT], F32R)
    ATL = at(32 * KB, [NT, HT], F32R)
    AF0 = at(0, [NT, HT])
    AF1 = at(32 * KB, [NT, HT])
    XF0 = at(64 * KB, [NT, HT])
    XF1 = at(96 * KB, [NT, HT])
    XL_ = at(64 * KB, [NT, HT], F32R)
    XH_ = at(96 * KB, [NT, HT], F32R)
    AL_ = ATL
    NR = 8
    RS = (CM * 4 + 63) // 64 * 64
    ring = [at(64 * KB + i * RS, [CM]) for i in range(NR)]
    o = 64 * KB + NR * RS
    Mb = []
    for i in range(3):
        Mb.append(at(o, [CM], BF16))
        o += 3232
    scr = at(o, [CM], BF16); o += 3232
    L4 = at(o, [2, NT, 4])
    dq = [at(o + 256 * y, [NT, 7], BF16) for y in range(2)]
    o += 512
    L2 = at(o, [2, NT, 2]); o += 256
    nT = at(o, [2, 2]); o += 32
    assert o <= 128 * KB, o
    G = ring[0]
    pend_ = at(64 * KB + RS + 3 * KB + 256, [1])
    w256 = at(64 * KB + RS, [256])
    oh = at(64 * KB + RS + KB, [256], U32)
    c64 = at(64 * KB + RS + 2 * KB, [64])
    eqb = at(64 * KB + RS + 2 * KB + 256, [64])
    prb = at(64 * KB + RS + 2 * KB + 512, [64])
    tk = at(64 * KB + RS + 2 * KB + 768, [40])
    sm = at(64 * KB + RS + 3 * KB, [16])
    idx = at(64 * KB + RS + 3 * KB + 64, [1], U32)
    fl2 = at(64 * KB + RS + 3 * KB + 128, [4])
    flu = at(64 * KB + RS + 3 * KB + 192, [2], U32)
    ke = at(64 * KB + 2 * RS, [NT, C], U32)
    kf2 = at(64 * KB + 3 * RS, [NT, C])
    crc = [at(96 * KB + i * 4 * KB, [NT, C]) for i in range(2)]
    sbc = [at(104 * KB + i * 4 * KB, [NT, C]) for i in range(2)]
    jnk = at(112 * KB, [C])
    Yp = at(113 * KB, [4 * B, 22])

    mask_off = top[0]
    kT = sb([4, HT])
    Vt = sb([4, HT])
    SB = [sb([HT]) for _ in range(2)]
    PTs = [sb([HT]) for _ in range(2)]
    qr_off = top[0]
    qr = [sb([HT]) for _ in range(2)]
    qs_off = top[0]
    qs = sb([HT])
    t1 = sb([HT])
    raw = [sb([4, 128]) for _ in range(4)]
    wh = [sb([4, 128], F32R) for _ in range(4)]
    wlo = [sb([4, 128], F32R) for _ in range(4)]
    rc = [sb([HT]) for _ in range(2)]
    ev = [sb([HT]) for _ in range(2)]
    assert top[0] - mask_off >= 64 * KB
    cand = at(mask_off, [B, NT, C])
    lsq = [at(mask_off + 60 * KB + 2 * KB * i, [HT]) for i in range(2)]
    gwr = at(mask_off + 56 * KB, [NT, 8])
    cst = sb([C_END])
    Mn = sb([HT])
    Rs = sb([HT])
    r1_off = top[0]
    R1 = sb([HT])
    thr = at(r1_off, [B, NT])
    cut = at(r1_off + KB, [B, NT])
    stat_off = top[0]
    stat = sb([4, B, NT])
    flg = at(stat_off, [B, NT])
    rid = at(stat_off + KB, [B, NT])
    v8 = at(stat_off + 2 * KB, [2, NT, 8])
    cnt = at(stat_off + 3 * KB, [3, 2, NT])
    ins = at(stat_off + 3 * KB + 384, [3, 2, NT], U32)
    identb = at(stat_off + 3 * KB + 768, [128], BF16)
    lgh = at(stat_off, [HT], F32R)
    lgl = at(stat_off + 2 * KB, [HT], F32R)
    t2 = at(qs_off, [HT])
    ggf = sb([16 * NT + 112], F32R)
    gg = ggf[:, 0:16 * NT].rearrange("p (t a n) -> p t a n", a=2, n=8)
    bbs = sb([NT])
    w16 = sb([16])
    sc = sb([80])
    assert top[0] <= nc.sbuf_usable_end - base, top[0]
    Z = at(113 * KB + 4 * B * 22 * 4, [2, 256])
    Zt = at(113 * KB + 4 * B * 22 * 4 + 2048, [2, 256])
    A12 = at(113 * KB + 4 * B * 22 * 4 + 4096, [2, 256])
    Dm = stat[:, 0, :, :]
    A2 = stat[:, 1, :, :]

    ps = [nc.alloc_psum_tensor(f"ps{i}", [128, 512], F32) for i in range(8)]
    PA, PS_, PT, PO = ps[0:3], ps[3], ps[4:6], ps[6:8]

    d_c = sem("d_c"); d_x = [sem("d_x0"), sem("d_x1")]
    d_r = [sem(f"d_r{i}") for i in range(NR)]
    d_w = [sem(f"d_w{i}") for i in range(4)]
    d_xr = [sem("d_xr0"), sem("d_xr1")]
    d_s = sem("d_s"); d_s2 = sem("d_s2"); d_rc = [sem("d_rc0"), sem("d_rc1")]
    d_o = [sem("d_o0"), sem("d_o1")]
    d_ln = sem("d_ln")

    ones = cst[:, C_ONES:C_ONES + 128]
    ident = cst[:, C_ID:C_ID + 128]

    k_c = Q.D("sync", d_c, cst[:, :], cst_d)
    k_c = Q.D("sync", d_c, w16[:, 0:14], cw)
    k_c = Q.D("sync", d_c, w16[:, 14:16], bn)
    k_c = Q.D("sync", d_c, bbs[:, :], bb)
    k_c = Q.D("sync", d_c, gwr[:, :, :], gw)
    k_c = Q.D("sync", d_c, rid[:, :, :], rn.rearrange("p (b t) -> p b t", t=NT))
    k_x = [Q.D("sync", d_x[h], XN[:, h, :, :], xT[:, h, :, :]) for h in range(2)]

    def over_t(ap):
        return ap.rearrange("p t n -> p n t")

    def bc(ap, n):
        return ap.rearrange("p (a n) -> p a n", a=1).to_broadcast([128, n, HT])

    def layernorm(x, scratch, bank, waits, bank_free):
        k = V(lambda e: e.tensor_reduce(R1[:, :], over_t(x[:, :, :]), AX.X, ALU.add), *waits)
        k = T(lambda e: e.matmul(bank[:, :], ones, R1[:, :], start=True, stop=True), k, bank_free, k_c)
        k = V(lambda e: e.tensor_scalar(Mn[:, :], bank[:, :], 1.0 / L, None, ALU.mult), k)
        a = V(lambda e: e.tensor_tensor(x[:, 0:11, :], x[:, 0:11, :], bc(Mn[:, :], 11), ALU.subtract), k)
        b = P(lambda e: e.tensor_tensor(x[:, 11:16, :], x[:, 11:16, :], bc(Mn[:, :], 5), ALU.subtract), k)
        k1 = A(lambda e: e.activation(scratch[:, 0:11, :], x[:, 0:11, :], ACT.Square), a)
        k2 = A(lambda e: e.activation(scratch[:, 11:16, :], x[:, 11:16, :], ACT.Square), b)
        k = V(lambda e: e.tensor_reduce(R1[:, :], over_t(scratch[:, :, :]), AX.X, ALU.add), k1, k2)
        k = T(lambda e: e.matmul(bank[:, :], ones, R1[:, :], start=True, stop=True), k)
        k = V(lambda e: e.tensor_scalar(Mn[:, :], bank[:, :], 1.0 / L, EPS, ALU.mult, ALU.add), k)
        bf = k
        k = A(lambda e: e.activation(R1[:, :], Mn[:, :], ACT.Sqrt), k)
        k = V(lambda e: e.reciprocal(Rs[:, :], R1[:, :]), k)
        return k, bf

    kgh = A(lambda e: e.activation(gg[:, :, 0, :], gwr[:, :, :], ACT.Copy), k_c)
    kgh = A(lambda e: e.activation(ggf[:, 16 * NT:], cst[:, 0:112], ACT.Copy), k_c)
    k_gw = V(lambda e: e.tensor_tensor(gg[:, :, 1, :], gwr[:, :, :], gg[:, :, 0, :].bitcast(F32), ALU.subtract), kgh)
    k_idb = V(lambda e: e.tensor_copy(identb[:, :], ident), k_c)

    def ln0():
        sq = [None, None]
        b0 = None
        for h in range(2):
            x = XN[:, h, :, :]

            def total_of(e, x=x):
                for t in range(NT):
                    m = e.matmul(ps[6][:, :], ones, x[:, t, :], start=(t == 0), stop=(t == NT - 1))
                return m
            k = T(total_of, k_x[h], k_c, b0)
            km = A(lambda e: e.activation(Mn[:, :], ps[6][:, :], ACT.Copy, scale=1.0 / L), k,
                   Q.last("gpsimd") if h else None)
            for t in range(NT):
                xt = x[:, t, :]
                k1 = P(lambda e, xt=xt: e.tensor_tensor(xt, xt, Mn[:, :], ALU.subtract), km)
                k2 = P(lambda e, xt=xt, t=t: e.tensor_tensor(lsq[t % 2][:, :], xt, xt, ALU.mult), k1, sq[t % 2])
                yield
                sq[t % 2] = T(lambda e, t=t: e.matmul(ps[7][:, :], ones, lsq[t % 2][:, :],
                                                      start=(t == 0), stop=(t == NT - 1)), k2, b0 if t == 0 else None)
            k = V(lambda e: e.tensor_scalar(Mn[:, :], ps[7][:, :], 1.0 / L, EPS, ALU.mult, ALU.add), sq[1])
            b0 = k
            k = A(lambda e: e.activation(Mn[:, :], Mn[:, :], ACT.Sqrt), k)
            k = V(lambda e: e.reciprocal(Rs[:, :], Mn[:, :]), k)
            for t in range(NT):
                xt = x[:, t, :]
                P(lambda e, xt=xt: e.tensor_tensor(xt, xt, Rs[:, :], ALU.mult), k)
                if t % 2:
                    yield
        yield

    NG = B * NT // 2
    bankf = [None] * 6
    bankn = [0]
    mbf = [None] * 3
    mbn = [0]
    freed = [[] for _ in range(NR)]
    kl, kA, kB, kC, kD, kv8 = {}, {}, {}, {}, {}, {}
    kcp = {}
    SHRINK = float(np.float32(1.0) - np.float32(2.0 ** -24))
    k_scr = [None]
    k_thr = V(lambda e: e.memset(thr[:, :, :], FMAX))
    k_cut = V(lambda e: e.memset(cut[:, :, :], float(C)))
    small_free = [[], []]

    def where(n):
        return n // NT % 2, n % NT

    def load(n):
        s = n % NR
        b, t = n // NT, n % NT
        kl[n] = Q.D("sync", d_r[s], ring[s][:, :], ctxT[b].rearrange("(p t) c -> p t c", t=NT)[:, t, :], *freed[s])

    def cand_copy(n):
        b, t = n // NT, n % NT
        kcp[n] = P(lambda e, n=n, b=b, t=t: e.tensor_copy(cand[:, (b + 8) % 16, t, :], ring[n % NR][:, 0:C]), kl[n],
                   k_gw if b == 6 else None, k_ln0[0] if b == 7 else None)

    kmx = {}

    def stage_a(g):
        for n in (2 * g, 2 * g + 1):
            y, t = where(n)
            kmx[g] = V(lambda e, n=n, y=y, t=t: e.max(v8[:, y, t, :], ring[n % NR][:, 0:C]), kl[n], *small_free[y])

    def start_of(g):
        y, t = where(2 * g)
        k = kmx[g]
        return V(lambda e, y=y, t=t, g=g: e.tensor_scalar(nT[:, g % 2, :], v8[:, y, t:t + 2, 3], TINY, -1.0,
                                                          ALU.max, ALU.mult), k, kA.get(g - 2))

    def signs(g, u, k):
        n = 2 * g + u
        y, t = where(n)
        kA[g] = k_scr[0] = A(lambda e, n=n, y=y, t=t, g=g: e.activation(
            scr[:, :], ring[n % NR][:, :], ACT.Sign, bias=nT[:, g % 2, n % 2:n % 2 + 1], scale=SHRINK,
            accum_out=cnt[:, 0, y, t:t + 1]), k, k_scr[0])

    def count(n, step, sc_ap, kw):
        m = mbn[0] % 3
        mbn[0] += 1
        q = bankn[0] % 6
        bankn[0] += 1
        y, t = where(n)
        k = V(lambda e, m=m, n=n: e.tensor_scalar(Mb[m][:, :], ring[n % NR][:, :], sc_ap, None, ALU.is_gt), kw, mbf[m])
        kc = k

        def fn(e, m=m, q=q):
            for c in range(13):
                w = min(128, CM - 128 * c)
                mm = e.matmul(ps[q][:, 0:w], identb[:, :], Mb[m][:, 128 * c:128 * c + w], start=(c == 0), stop=(c == 12))
            return mm
        k = T(fn, k, bankf[q], k_idb)
        mbf[m] = k
        return q, k, kc, (y, t, step)

    def gather_counts(lst):
        for q, k, _, (y, t, step) in lst:
            k_scr[0] = bankf[q] = A(lambda e, q=q, y=y, t=t, step=step: e.activation(
                scr[:, 0:128], ps[q][:, 0:128], ACT.Copy, accum_out=cnt[:, step, y, t:t + 1]), k, k_scr[0])
        return k_scr[0]

    def narrow(y, t, step, bound, kin, dst, src, half, between):
        k = V(lambda e: e.tensor_scalar(ins[:, step, y, t:t + 2], cnt[:, step, y, t:t + 2], bound, None, ALU.is_lt), kin)
        V(lambda e: e.tensor_copy(dst, src[:, :, 0:half]))
        k = Q.last("vector")
        between()
        w = ins[:, step, y, t:t + 2].rearrange("p (a n) -> p a n", n=1).to_broadcast([128, 2, half])
        k = V(lambda e: e.copy_predicated(dst, w, src[:, :, half:2 * half]), k)
        fill()
        return k

    d_steps = [None]

    def fill(n=1):
        for _ in range(n):
            if d_steps[0] is not None and next(d_steps[0], 1) == 1:
                d_steps[0] = None

    cB, cC = {}, {}

    def narrow_b(g, between):
        y, t = where(2 * g)
        return narrow(y, t, 0, 2.0 * K - CM - 1.0, kA[g], L4[:, y, t:t + 2, :], v8[:, y, t:t + 2, :], 4, between)

    def count_b(g, u, k):
        n = 2 * g + u
        y, t = where(n)
        cB[g, u] = count(n, 1, L4[:, y, t, 1:2], k)

    def narrow_c(g):
        y, t = where(2 * g)
        return narrow(y, t, 1, float(K), kB[g], L2[:, y, t:t + 2, :], L4[:, y, t:t + 2, :], 2, fill)

    def count_c(g, u, k):
        n = 2 * g + u
        y, t = where(n)
        cC[g, u] = count(n, 2, L2[:, y, t, 0:1], k)
        freed[n % NR] = [cC[g, u][2], kcp[n]]
        if n + NR < B * NT:
            load(n + NR)

    k_d = [None]

    def stage_d(b):
        y = b % 2
        i1, i2, i3 = (ins[:, s_, y, :] for s_ in range(3))
        v4, f = v8[:, y, :, 3], flg[:, b, :]
        k = V(lambda e: e.tensor_scalar(i3, cnt[:, 2, y, :], float(K), None, ALU.is_lt), kC[(b + 1) * NT // 2 - 1])
        yield
        k = V(lambda e: e.copy_predicated(thr[:, b, :], i1, v4), k)
        yield
        k = V(lambda e: e.copy_predicated(thr[:, b, :], i2, L4[:, y, :, 1]), k)
        yield
        k = V(lambda e: e.copy_predicated(thr[:, b, :], i3, L2[:, y, :, 0]), k)
        yield
        r0, r1 = cnt[:, 0, y, :], cnt[:, 1, y, :]
        e7 = dq[y]
        k = V(lambda e: e.tensor_tensor(f, i1, i2, ALU.mult), k)
        yield
        k = V(lambda e: e.tensor_tensor(f, f, i3, ALU.mult), k)
        yield
        k = V(lambda e: e.scalar_tensor_tensor(r0, v4, TINY, i1, ALU.is_lt, ALU.mult), k)
        yield
        k = V(lambda e: e.tensor_tensor(f, f, r0, ALU.max), k)
        yield
        k = V(lambda e: e.tensor_scalar(i1, v4.bitcast(U32), 0x7FFFFF, None, ALU.bitwise_and), k)
        yield
        k = V(lambda e: e.tensor_scalar(r0, i1, float(0x7FFFFF), None, ALU.is_equal), k)
        yield
        k = V(lambda e: e.tensor_tensor(f, f, r0, ALU.max), k)
        yield
        k = V(lambda e: e.tensor_tensor(e7[:, :, :], v8[:, y, :, 0:7], v8[:, y, :, 1:8], ALU.is_equal), k)
        yield
        k = V(lambda e: e.tensor_reduce(r1, e7[:, :, :], AX.X, ALU.max), k)
        yield
        k = V(lambda e: e.tensor_tensor(f, f, r1, ALU.max), k)
        small_free[y] = [k]
        k_d[0] = k
        yield

    bg = ln0()
    k_ln0 = [None]
    next_load = 0
    for n in range(NR):
        load(n)
    next_load = NR
    sx = [0]

    def sum_xn():
        for hc in range(2 * C):
            h, c = hc // C, hc % C
            src = XN[:, h, :, :].rearrange("p t (b c) -> p c b t", c=C)[:, c]
            dst = ps[6][:, 128 * h:128 * h + 128].rearrange("p (b t) -> p b t", t=NT)
            k_sx[0] = T(lambda e, dst=dst, src=src, c=c: e.matmul(dst, cst[:, C_ID:C_ID + 128], src, start=(c == 0),
                                                                  stop=(c == C - 1)), k_ln0[0])
            if c % 4 == 3:
                yield
    k_sx = [None]
    sxg = None
    for i in range(NG + 3):
        if i < NG:
            if i % 8 == 0:
                fill(20)
            stage_a(i)
            cand_copy(2 * i)
            cand_copy(2 * i + 1)
        ka_ = [None]

        def begin(i=i, ka_=ka_):
            if i < NG:
                ka_[0] = start_of(i)
            else:
                fill()
        if 1 <= i <= NG:
            kn = narrow_b(i - 1, begin)
        else:
            begin()
        if i < NG:
            signs(i, 0, ka_[0])
        if bg is None and i % 2 and sxg is not None:
            next(sxg, 1)
        for _ in range(2):
            if bg is not None and next(bg, 1) == 1:
                bg = None
                k_ln0[0] = Q.last("gpsimd")
                sxg = sum_xn()
        if 1 <= i <= NG:
            count_b(i - 1, 0, kn)
            gather_counts([cB[i - 1, 0]])
        if i < NG:
            signs(i, 1, ka_[0])
        if 2 <= i <= NG + 1:
            kc_ = narrow_c(i - 2)
            count_c(i - 2, 0, kc_)
            count_c(i - 2, 1, kc_)
        if 1 <= i <= NG:
            count_b(i - 1, 1, kn)
        if 2 <= i <= NG + 1:
            kC[i - 2] = gather_counts([cC[i - 2, 0], cC[i - 2, 1]])
        if 1 <= i <= NG:
            kB[i - 1] = gather_counts([cB[i - 1, 1]])
        if i >= 3 and (i - 3) % 8 == 7:
            fill(20)
            d_steps[0] = stage_d((i - 3) // 8)
    for _ in sxg:
        pass
    fill(20)
    k_srch = k_d[0]
    k_scp = Q.last("gpsimd")

    f_s, h_s, g_s, gd_s, w_s = sem("f_s"), sem("h_s"), sem("g_s"), sem("gd_s"), sem("w_s")
    rows = ctxT.rearrange("b l c -> (b l) c")

    def chain(e):
        n = [0]

        def do(ins_):
            n[0] += 1
            ins_.then_inc(w_s, 1)
            e.wait_ge(w_s, n[0])
        return do

    thf, ctf, flf, rif = (x_[:, :, :].rearrange("p b t -> p (b t)") for x_ in (thr, cut, flg, rid))

    def pick(e, do):
        do(e.tensor_reduce(fl2[:, 0:1], flf, AX.X, ALU.max))
        do(e.tensor_tensor(w256[:, :], flf, rif, ALU.mult))
        do(e.tensor_reduce(sm[:, 8:9], w256[:, :], AX.X, ALU.max))
        do(e.tensor_scalar(sm[:, 9:10], sm[:, 8:9], -1.0, 0.0, ALU.add, ALU.max))
        do(e.tensor_copy(idx[:, :], sm[:, 9:10]))
        e.sem_clear(w_s)
        e.sem_inc(f_s, 1)

    def open_rows_v(e):
        do = chain(e)
        do(e.memset(fl2[:, :], 0.0))
        do(e.memset(sm[:, 10:11], -FMAX))
        do(e.memset(sm[:, 11:12], 0.0))
        pick(e, do)

        def head():
            e.wait_ge(h_s, 1)
            e.sem_clear(h_s)
            return e.value_load(flu[0:1, 0:1])
        with e.While(head):
            e.wait_ge(gd_s, 1)
            e.sem_clear(gd_s)
            do = chain(e)
            do(e.tensor_copy(c64[:, :], G[:, 0:C]))
            for r in range(5):
                do(e.max(tk[:, 8 * r:8 * r + 8], G[:, :]))
                if r < 4:
                    do(e.match_replace(G[:, :], tk[:, 8 * r:8 * r + 8], G[:, :], -FMAX))
            T38 = tk[:, K - 1:K]
            do(e.tensor_scalar(w256[:, 0:40], tk[:, :], T38, None, ALU.is_gt, ALU.add, accum_out=sm[:, 0:1]))
            do(e.tensor_scalar(sm[:, 1:2], sm[:, 0:1], -1.0, float(K), ALU.mult, ALU.add))
            do(e.tensor_scalar(eqb[:, :], c64[:, :], T38, None, ALU.is_equal))
            do(e.tensor_tensor_scan(prb[:, :], cst[:, C_ONES:C_ONES + C], eqb[:, :], 0.0, ALU.mult, ALU.add))
            do(e.tensor_scalar(eqb[:, :], prb[:, :], sm[:, 1:2], None, ALU.is_le, ALU.add, accum_out=sm[:, 2:3]))
            do(e.tensor_scalar(sm[:, 3:4], sm[:, 2:3], float(C), None, ALU.is_lt))
            do(e.tensor_tensor(fl2[:, 1:2], fl2[:, 1:2], sm[:, 3:4], ALU.max))
            do(e.tensor_scalar(oh[:, :], rif, sm[:, 8:9], None, ALU.is_equal))
            do(e.copy_predicated(thf, oh[:, :], T38.to_broadcast([128, 256])))
            do(e.copy_predicated(ctf, oh[:, :], sm[:, 2:3].to_broadcast([128, 256])))
            do(e.copy_predicated(flf, oh[:, :], sm[:, 11:12].to_broadcast([128, 256])))
            pick(e, do)
        with e.If(e.value_load(flu[0:1, 1:2])):
            do = chain(e)
            for b in range(B):
                cb = cand[:, (b + 8) % 16, :, :]
                tb = thr[:, b, :].rearrange("p (t a) -> p t a", a=1).to_broadcast([128, NT, C])
                ub = cut[:, b, :].rearrange("p (t a) -> p t a", a=1).to_broadcast([128, NT, C])
                io = cst[:, C_IOTA:C_IOTA + C].rearrange("p (a c) -> p a c", a=1).to_broadcast([128, NT, C])
                do(e.tensor_tensor(kf2[:, :, :], cb, tb, ALU.is_equal))
                do(e.tensor_tensor(ke[:, :, :], io, ub, ALU.is_ge))
                do(e.tensor_tensor(ke[:, :, :], ke[:, :, :], kf2[:, :, :], ALU.mult))
                do(e.copy_predicated(cb, ke[:, :, :], sm[:, 10:11].rearrange("p (a n) -> p a n", n=1)
                                     .to_broadcast([128, NT, C])))
            e.sem_clear(w_s)
        return e.tensor_copy(sm[:, 12:13], sm[:, 11:12])

    def open_rows_p(e):
        def head():
            e.wait_ge(f_s, 1)
            e.sem_clear(f_s)
            e.partition_all_reduce(fl2[:, 2:4], fl2[:, 0:2], 128, bass.bass_isa.ReduceOp.max).then_inc(g_s, 1)
            e.wait_ge(g_s, 1)
            e.tensor_copy(flu[:, :], fl2[:, 2:4]).then_inc(g_s, 1)
            e.wait_ge(g_s, 2)
            e.sem_clear(g_s)
            e.sem_inc(h_s, 1)
            return e.value_load(flu[0:1, 0:1])
        with e.While(head):
            e.indirect_dma_start(G[:, :], None, rows, bass.IndirectOffsetOnAxis(ap=idx[:, 0:1], axis=0))\
                .then_inc(d_g, 16)
            e.wait_ge(d_g, 16)
            e.dma_reset(range(d_g.num, d_g.num + 1))
            e.sem_clear(d_g)
            e.sem_inc(gd_s, 1)
        return e.memset(pend_[:, :], 0.0)

    d_g = sem("d_g")
    k_open = V(open_rows_v, k_srch, k_scr[0], k_scp, Q.last("tensor"))
    k_pool = P(open_rows_p)

    k_xrA = Q.D("sync", d_xr[0], XF0[:, :, :], xT[:, 0, :, :], k_open, k_pool)

    cb_free = [None, None]
    k_st = []
    for b in range(B):
        y = b % 2
        xb = XN[:, b // HB, :, (b % HB) * C:(b % HB) * C + C]
        cb = cand[:, (b + 8) % 16, :, :]
        tb = thr[:, b, :].rearrange("p (t a) -> p t a", a=1).to_broadcast([128, NT, C])
        k = V(lambda e, cb=cb, tb=tb: e.tensor_tensor(cb, cb, tb, ALU.is_ge), k_open, k_pool)
        k1 = (V if b % 4 == 3 else P)(lambda e, xb=xb, cb=cb, y=y: e.tensor_tensor(crc[y][:, :, :], cb, xb, ALU.mult),
                                      k, *(cb_free[y] or []))
        k2 = P(lambda e, xb=xb, y=y: e.tensor_tensor(sbc[y][:, :, :], xb, crc[y][:, :, :], ALU.subtract), k1,
               *(cb_free[y] or []))
        for t in range(NT):
            ka = A(lambda e, b=b, y=y, t=t: e.activation(jnk[:, :], crc[y][:, t, :], ACT.Copy,
                                                         accum_out=stat[:, 2, b, t:t + 1]), k1, k_scr[0])
            k_scr[0] = ka
        k_st.append((b, y, k1, k2, ka))
        for (b_, y_, k1_, k2_, ka_) in (k_st[b - 1:b] if b >= 1 else []) + (k_st[b:] if b == B - 1 else []):
            V(lambda e, b=b_, y=y_: e.tensor_reduce(stat[:, 0, b, :], crc[y][:, :, :], AX.X, ALU.max), k1_)
            k_cs = V(lambda e, b=b_, y=y_: e.tensor_reduce(stat[:, 1, b, :], sbc[y][:, :, :], AX.X, ALU.max), k2_)
            cb_free[y_] = [k_cs, ka_]
    k_cs2 = k_scr[0]
    k_cs = V(lambda e: e.tensor_tensor(stat[:, 3, :, :], ps[6][:, 0:256].rearrange("p (b t) -> p b t", t=NT),
                                       stat[:, 2, :, :], ALU.subtract), k_sx[0], k_cs2)

    Y4 = Yp[:, :, :].rearrange("p (f b) t -> p f b t", f=4)
    k = V(lambda e: e.tensor_scalar(stat[:, 2, :, :], stat[:, 2, :, :], 1.0 / C, C / K, ALU.mult, ALU.mult), k_cs, k_cs2)
    k = V(lambda e: e.tensor_scalar(stat[:, 3, :, :], stat[:, 3, :, :], 1.0 / C, C / (C - K), ALU.mult, ALU.mult), k)
    st = stat[:, :, :, :].rearrange("p f b t -> p (f b) t")
    kk = V(lambda e: e.tensor_copy(Yp[:, :, 3:19], st), k)
    kl = T(lambda e: e.matmul(PA[1][:, 0:192].rearrange("p (g t) -> p g t", t=3), cst[:, C_SHL:C_SHL + 128],
                              st[:, :, 13:16], start=True, stop=True), k)
    kr = T(lambda e: e.matmul(PA[2][:, 0:192].rearrange("p (g t) -> p g t", t=3), cst[:, C_SHR:C_SHR + 128],
                              st[:, :, 0:3], start=True, stop=True), k)
    kl = V(lambda e: e.tensor_copy(Yp[:, :, 0:3], PA[1][:, 0:192].rearrange("p (g t) -> p g t", t=3)), kl)
    k = V(lambda e: e.tensor_copy(Yp[:, :, 19:22], PA[2][:, 0:192].rearrange("p (g t) -> p g t", t=3)), kr)
    Zf = Z[:, :, :].rearrange("p s (b t) -> p (s b) t", t=NT)
    for ch in range(2):
        for tap in range(7):
            src = Yp[:, ch * 32:ch * 32 + 32, tap:tap + 16]
            wsc = w16[:, ch * 7 + tap:ch * 7 + tap + 1]
            if ch == 0 and tap == 0:
                k = V(lambda e, src=src, wsc=wsc: e.tensor_scalar(Zf, src, wsc, None, ALU.mult), k, k_c)
            else:
                k = V(lambda e, src=src, wsc=wsc: e.scalar_tensor_tensor(Zf, src, wsc, Zf, ALU.mult, ALU.add), k)

    def total(src, col):
        k1 = V(lambda e: e.tensor_reduce(sc[:, col + 2:col + 4], src, AX.X, ALU.add), k)
        k2 = T(lambda e: e.matmul(PA[1][:, 0:2], ones, sc[:, col + 2:col + 4], start=True, stop=True), k1)
        return V(lambda e: e.tensor_scalar(sc[:, col:col + 2], PA[1][:, 0:2], 1.0 / (B * L), None, ALU.mult), k2)

    k = total(Z[:, :, :], 0)
    for s in range(2):
        k = V(lambda e, s=s: e.tensor_scalar(Z[:, s, :], Z[:, s, :], sc[:, s:s + 1], None, ALU.subtract), k)
    k = V(lambda e: e.tensor_tensor(Zt[:, :, :], Z[:, :, :], Z[:, :, :], ALU.mult), k)
    k = total(Zt[:, :, :], 4)
    k = V(lambda e: e.tensor_scalar(sc[:, 8:10], sc[:, 4:6], EPS, None, ALU.add), k)
    k = A(lambda e: e.activation(sc[:, 10:12], sc[:, 8:10], ACT.Sqrt), k)
    k = V(lambda e: e.reciprocal(sc[:, 12:14], sc[:, 10:12]), k)
    for s in range(2):
        k = V(lambda e, s=s: e.tensor_scalar(Z[:, s, :], Z[:, s, :], sc[:, 12 + s:13 + s], w16[:, 14:15],
                                             ALU.mult, ALU.mult), k)
    k = V(lambda e: e.tensor_scalar(Z[:, :, :], Z[:, :, :], w16[:, 15:16], 0.0, ALU.add, ALU.max), k)
    k = A(lambda e: e.activation(Zt[:, :, :], Z[:, :, :], ACT.Exp, scale=-1.0), k)
    k = V(lambda e: e.tensor_scalar(Zt[:, :, :], Zt[:, :, :], 1.0, None, ALU.add), k)
    k = V(lambda e: e.reciprocal(A12[:, :, :], Zt[:, :, :]), k)
    k = V(lambda e: e.tensor_tensor(Dm, A12[:, 0, :].rearrange("p (b t) -> p b t", t=NT),
                                    A12[:, 1, :].rearrange("p (b t) -> p b t", t=NT), ALU.subtract), k)
    k_g = V(lambda e: e.tensor_copy(A2, A12[:, 1, :].rearrange("p (b t) -> p b t", t=NT)), k)

    def gated(b, eng=P):
        h = b // HB
        xb = XN[:, h, :, (b % HB) * C:(b % HB) * C + C]
        u = cand[:, (b + 8) % 16, :, :]
        nt = NT // 2
        dm = Dm[:, b, nt:].rearrange("p (t a) -> p t a", a=1).to_broadcast([128, NT - nt, C])
        a2 = A2[:, b, nt:].rearrange("p (t a) -> p t a", a=1).to_broadcast([128, NT - nt, C])
        for t in range(nt):
            ka = A(lambda e, t=t: e.activation(u[:, t, :], u[:, t, :], ACT.Identity, scale=Dm[:, b, t:t + 1],
                                               bias=A2[:, b, t:t + 1]), k_g)
        k = V(lambda e: e.tensor_tensor(u[:, nt:, :], u[:, nt:, :], dm, ALU.mult), k_g)
        k = V(lambda e: e.tensor_tensor(u[:, nt:, :], u[:, nt:, :], a2, ALU.add), k)
        return u, P(lambda e: e.tensor_tensor(u, u, xb, ALU.mult), k, ka)

    def pair(x, q):
        return x[:, :, 128 * q:128 * q + 128]

    def bcp(ap, q):
        return ap[:, 128 * q:128 * q + 128].rearrange("p (a n) -> p a n", a=1).to_broadcast([128, NT, 128])

    def sums(src, q, k):
        def fn(e):
            for t in range(NT):
                m = e.matmul(ps[q][:, 0:128], ones, src[:, t, 128 * q:128 * q + 128], start=(t == 0), stop=(t == NT - 1))
            return m
        return T(fn, *k)
    gt_, kx1, kst, kms, kr1, kl1_ = {}, {}, {}, {}, {}, {}
    d_sp = [sem(f"d_sp{q}") for q in range(4)]
    for i in range(4 + 3):
        if i < 4:
            for b in (2 * i, 2 * i + 1):
                gt_[b] = gated(b)
        if 1 <= i < 5:
            q = i - 1
            for b in (2 * q, 2 * q + 1):
                u, k = gt_[b]
                x = XF0[:, :, b * C:b * C + C]
                kx1[q] = V(lambda e, u=u, x=x: e.tensor_tensor(x, x, u, ALU.add), k, k_xrA)
            kst[q] = Q.D("sync", d_sp[q], pair(x1d[:, 0, :, :], q), pair(XF0, q), kx1[q])
            k = sums(XF0, q, [kx1[q]])
            km = A(lambda e, q=q: e.activation(Mn[:, 128 * q:128 * q + 128], ps[q][:, 0:128], ACT.Copy,
                                               scale=1.0 / L), k)
        if 2 <= i < 6:
            q = i - 2
            k = V(lambda e, q=q: e.tensor_tensor(pair(XF1, q), pair(XF0, q), bcp(Mn, q), ALU.subtract), kms[q])
            k = A(lambda e, q=q: e.activation(pair(AF0, q), pair(XF1, q), ACT.Square), k)
            k = sums(AF0, q, [k])
            k_sqd = k
            k = V(lambda e, q=q: e.tensor_scalar(Rs[:, 128 * q:128 * q + 128], ps[q][:, 0:128], 1.0 / L, EPS,
                                                 ALU.mult, ALU.add), k)
            k = A(lambda e, q=q: e.activation(Rs[:, 128 * q:128 * q + 128], Rs[:, 128 * q:128 * q + 128], ACT.Sqrt), k)
            kr1[q] = V(lambda e, q=q: e.reciprocal(Rs[:, 128 * q:128 * q + 128], Rs[:, 128 * q:128 * q + 128]), k)
        if 1 <= i < 5:
            kms[i - 1] = km
        if 3 <= i:
            q = i - 3
            k = V(lambda e, q=q: e.tensor_tensor(pair(XF1, q), pair(XF1, q), bcp(Rs, q), ALU.mult), kr1[q])
            k = A(lambda e, q=q: e.activation(pair(XL_, q), pair(XF1, q), ACT.Copy), k, kst[q])
            kl1_[q] = (V if q == 3 else P)(lambda e, q=q: e.tensor_tensor(
                pair(XH_, q), pair(XF1, q), pair(XL_, q).bitcast(F32), ALU.subtract), k)
    r1 = [kl1_[3], kl1_[2]]
    k_x1A = kx1[3]
    k_pa = [kr1[0], kr1[1], kr1[2]]
    k_p3 = kr1[3]

    k_x1B = [None]
    k_sx1 = (d_s, 64)

    def second_half(k_xrB):
        prev = None
        for b in range(HB, B + 1):
            cur = gated(b) if b < B else None
            if prev:
                u, k = prev
                x = AF0[:, :, (b - 1 - HB) * C:(b - HB) * C]
                k_x1B[0] = V(lambda e, u=u, x=x: e.tensor_tensor(x, x, u, ALU.add), k, k_xrB)
            prev = cur
            if b % 2 == 0 and HB < b < B:
                yield
        for c in range(4):
            yield
            yield
            Q.D("sync", d_s, x1d[:, 1, 4 * c:4 * c + 4, :], AF0[:, 4 * c:4 * c + 4, :], k_x1B[0])

    NH_ = len(wh)
    wst = {"n": 0, "raw": [k_x1A] * 4, "wf": [k_x1A] * NH_}

    def chunk(src, nk):
        n = wst["n"]
        wst["n"] += 1
        r, s = n % 4, n % NH_
        k = Q.D("sync", d_w[r], raw[r][:, 0:nk, :], src, wst["raw"][r])
        rr, hh, ll = raw[r][:, 0:nk, :], wh[s][:, 0:nk, :], wlo[s][:, 0:nk, :]
        k = A(lambda e: e.activation(hh, rr, ACT.Copy), k, wst["wf"][s])
        k = P(lambda e: e.tensor_tensor(ll, rr, hh.bitcast(F32), ALU.subtract), k, wst["wf"][s])
        wst["raw"][r] = k
        return s, k

    pend = []

    def order(items):
        for it in items:
            pend.append(it)

    AHEAD = 2
    ready = []

    def feed():
        while pend and len(ready) < AHEAD + 1:
            ready.append(chunk(*pend.pop(0)))

    pa_free = list(k_pa)
    pan = [0]

    steps = []

    def step():
        while steps:
            if next(steps[0], 1) == 1:
                steps.pop(0)
            else:
                return

    def project(X, xk, extra=None, hooks={}, x3=None):
        i = pan[0] % 3
        pan[0] += 1
        bank = PA[i]
        XHx, XLx = X
        total_ = 4 + (1 if extra else 0)
        for c in range(total_):
            feed()
            s, kw = ready.pop(0)
            nk = 4 if c < 4 else 1

            def fn(e, c=c, s=s, nk=nk):
                for q in range(nk):
                    kt = 4 * c + q
                    xh, xl = (XHx[:, kt, :], XLx[:, kt, :]) if c < 4 else (extra[0][:, :], extra[1][:, :])
                    e.matmul(bank[:, :], wh[s][:, q, :], xl, start=(c == 0 and q == 0), stop=False)
                    e.matmul(bank[:, :], wlo[s][:, q, :], xh, start=False, stop=False)
                    m = e.matmul(bank[:, :], wh[s][:, q, :], xh, start=False, stop=(c == total_ - 1 and q == nk - 1))
                return m
            k = T(fn, kw, *(xk if c == 0 else []), pa_free[i] if c == 0 else None, extra[2] if c == 4 else None,
                  x3[0] if x3 and c == 3 else None)
            wst["wf"][s] = k
            feed()
            step()
            for f in hooks.get(c, ()):
                f()
        return i, bank, k

    def wblock(w, nb, extra=False):
        src = w[nb]
        out_ = [(src[:, 4 * c:4 * c + 4, :], 4) for c in range(4)]
        if extra:
            out_.append((src[:, 16:17, :], 1))
        return out_

    def later(n, gen):
        for _ in range(n):
            yield
        yield from gen

    def ln_load(dst, src, waits):
        ln_wait[:] = [Q.D("sync", d_ln, dst, src, *waits)]
        for _ in range(8):
            yield

    ln_wait = []

    def ln_steps(x, sq, hi, lo_, wait, out_):
        bank, free = PT[0], st_["PT"][0]

        def reduce_t(src, w):
            for c in range(2):
                cs = slice(256 * c, 256 * c + 256)
                k = V(lambda e, cs=cs: e.tensor_reduce(R1[:, cs], over_t(src[:, :, cs]), AX.X, ALU.add), *(w or ln_wait))
                yield
            w[:] = [k]
        w = [wait] if wait else []
        yield from reduce_t(x, w)
        k = T(lambda e: e.matmul(bank[:, :], ones, R1[:, :], start=True, stop=True), w[0], free)
        yield
        k = V(lambda e: e.tensor_scalar(Mn[:, :], bank[:, :], 1.0 / L, None, ALU.mult), k)
        ks = []
        for c in range(4):
            k1 = V(lambda e, c=c: e.tensor_tensor(x[:, 4 * c:4 * c + 4, :], x[:, 4 * c:4 * c + 4, :],
                                                  bc(Mn[:, :], 4), ALU.subtract), k)
            yield
            ks.append(A(lambda e, c=c: e.activation(sq[:, 4 * c:4 * c + 4, :], x[:, 4 * c:4 * c + 4, :],
                                                    ACT.Square), k1))
        w = [ks[-1]]
        yield
        yield from reduce_t(sq, w)
        k = T(lambda e: e.matmul(bank[:, :], ones, R1[:, :], start=True, stop=True), w[0])
        yield
        k = V(lambda e: e.tensor_scalar(Mn[:, :], bank[:, :], 1.0 / L, EPS, ALU.mult, ALU.add), k)
        st_["PT"][0] = k
        k = A(lambda e: e.activation(R1[:, :], Mn[:, :], ACT.Sqrt), k)
        yield
        k = V(lambda e: e.reciprocal(Rs[:, :], R1[:, :]), k)
        for c in range(5):
            if c < 4:
                k1 = V(lambda e, c=c: e.tensor_tensor(x[:, 4 * c:4 * c + 4, :], x[:, 4 * c:4 * c + 4, :],
                                                      bc(Rs[:, :], 4), ALU.mult), k)
                k2 = A(lambda e, c=c: e.activation(hi[:, 4 * c:4 * c + 4, :], x[:, 4 * c:4 * c + 4, :], ACT.Copy), k1)
            if c > 0:
                out_[:] = [V(lambda e, c=c - 1: e.tensor_tensor(lo_[:, 4 * c:4 * c + 4, :], x[:, 4 * c:4 * c + 4, :],
                                                                hi[:, 4 * c:4 * c + 4, :].bitcast(F32),
                                                                ALU.subtract), kp)]
            kp = k2
            yield

    maskc = cst[:, C_MASK:C_MASK + 64].rearrange("p (a n) -> p a n", a=1).to_broadcast([128, 8, 64])
    swap = [i ^ 1 for i in range(32)]

    def rope(dst, bank, k, dst_free):
        cosb = cst[:, C_COS:C_COS + 64].rearrange("p (a n) -> p a n", a=1).to_broadcast([128, 8, 64])
        sinb = cst[:, C_SIN:C_SIN + 64].rearrange("p (a n) -> p a n", a=1).to_broadcast([128, 8, 64])

        def v3(ap):
            return ap.rearrange("p (a n) -> p a n", n=64)
        a = V(lambda e: e.stream_shuffle(qs[:, :], bank[:, :], swap), k, rope_free[0])
        b_ = V(lambda e: e.tensor_tensor(v3(t1[:, :]), v3(bank[:, :]), cosb, ALU.mult), k, rope_free[0])
        c = P(lambda e: e.tensor_tensor(v3(qs[:, :]), v3(qs[:, :]), sinb, ALU.mult), a)
        d = P(lambda e: e.tensor_tensor(dst, t1[:, :], qs[:, :], ALU.add), b_, c, dst_free)
        rope_free[0] = d
        return d, b_

    rope_free = [None]
    st_ = {"S": k_p3, "PT": [None] * 2, "O": None, "SB": [None] * 2, "PTs": [None] * 2, "qr": [None] * 2}

    def qk_scores(i, kq, kk_):
        j, s = i // 4, i % 2

        def fn(e):
            for bb_ in range(HB):
                for hf in range(2):
                    r = slice(64 * hf, 64 * hf + 64)
                    c = slice(64 * bb_, 64 * bb_ + 64)
                    m = e.matmul(PS_[r, c], qr[s][r, c], kT[r, j, c], start=True, stop=True)
            return m
        k = T(fn, kq, kk_, st_["S"])
        st_["qr"][s] = k
        p3 = SB[s][:, :].rearrange("p (a n) -> p a n", n=64)
        s3 = PS_[:, :].rearrange("p (a n) -> p a n", n=64)
        b0 = 16 + s * 32
        k = V(lambda e: e.scalar_tensor_tensor(p3, s3, 0.125, maskc, ALU.mult, ALU.add), k, st_["SB"][s])
        st_["S"] = k
        k = V(lambda e: e.tensor_reduce(sc[:, b0:b0 + 8], p3, AX.X, ALU.max), k)
        mx = sc[:, b0:b0 + 8].rearrange("p (a n) -> p a n", n=1).to_broadcast([128, 8, 64])
        k = V(lambda e: e.tensor_tensor(p3, p3, mx, ALU.subtract), k)
        k = A(lambda e: e.activation(SB[s][:, :], SB[s][:, :], ACT.Exp), k)
        k = V(lambda e: e.tensor_reduce(sc[:, b0 + 8:b0 + 16], p3, AX.X, ALU.add), k)
        k = V(lambda e: e.reciprocal(sc[:, b0 + 16:b0 + 24], sc[:, b0 + 8:b0 + 16]), k)
        rr = sc[:, b0 + 16:b0 + 24].rearrange("p (a n) -> p a n", n=1).to_broadcast([128, 8, 64])
        return V(lambda e: e.tensor_tensor(p3, p3, rr, ALU.mult), k)

    def transpose_p(i, tok):
        s = i % 2

        def fn(e):
            for pr in range(4):
                m = e.transpose(PT[s][:, pr * 128:pr * 128 + 128], SB[s][:, pr * 128:pr * 128 + 128], ident)
            return m
        k = T(fn, tok, st_["PT"][s])
        st_["SB"][s] = k
        k = A(lambda e: e.activation(PTs[s][:, :], PT[s][:, :], ACT.Copy), k, st_["PTs"][s])
        st_["PT"][s] = k
        return k

    def times_v(i, tok, kv, at_free):
        j, s = i // 4, i % 2

        def fn(e):
            for bb_ in range(HB):
                pr, r = bb_ // 2, slice(64 * (bb_ % 2), 64 * (bb_ % 2) + 64)
                for hf in range(2):
                    m = e.matmul(PO[bb_ % 2][64 * hf:64 * hf + 64, 64 * pr:64 * pr + 64],
                                 Vt[r, pr, (2 * j + hf) * 64:(2 * j + hf) * 64 + 64],
                                 PTs[s][r, pr * 128 + 64 * hf:pr * 128 + 64 * hf + 64], start=True, stop=True)
            return m
        k = T(fn, tok, kv, st_["O"])
        st_["PTs"][s] = k
        for z in range(2):
            hi = ATH[:, i, :].rearrange("p (a z n) -> p z a n", z=2, n=64)[:, z]
            lo_ = ATL[:, i, :].rearrange("p (a z n) -> p z a n", z=2, n=64)[:, z]
            src = PO[z][:, 0:256].rearrange("p (a n) -> p a n", n=64)
            a = A(lambda e, hi=hi, src=src: e.activation(hi, src, ACT.Copy), k, at_free)
            b_ = V(lambda e, hi=hi, lo_=lo_, src=src: e.tensor_tensor(lo_, src, hi.bitcast(F32), ALU.subtract), a)
        st_["O"] = b_
        return b_

    def qkv_attention(X, xk, region_free, at_free):
        kks, kvs = [], []
        for j in range(4):
            i, bank, k = project(X, xk)
            rope_free[0] = rope_free[0] or region_free[0]
            kd, bf_ = rope(kT[:, j, :], bank, k, region_free[0])
            pa_free[i] = bf_
            kks.append(kd)

        def vturn(j, kx):
            def fn(e):
                for tb in range(4):
                    m = e.transpose(PT[j % 2][:, tb * 128:tb * 128 + 128], SB[j % 2][:, tb * 128:tb * 128 + 128], ident)
                return m
            k = T(fn, kx, st_["PT"][j % 2])
            st_["SB"][j % 2] = k
            k = V(lambda e: e.tensor_copy(Vt[:, :, j * 128:j * 128 + 128],
                                          PT[j % 2][:, :].rearrange("p (a n) -> p a n", n=128)), k, region_free[0])
            st_["PT"][j % 2] = k
            kvs.append(k)
        vt = None
        for j in range(4):
            i, bank, k = project(X, xk, hooks={1: [lambda: vturn(*vt)]} if vt else {})
            kx = V(lambda e, j=j, bank=bank: e.tensor_copy(SB[j % 2][:, :], bank[:, :]), k, st_["SB"][j % 2], region_free[0])
            pa_free[i] = kx
            vt = (j, kx)
        kq, sco, pts = {}, {}, {}
        last = [None]

        def turn(i):
            pts[i] = transpose_p(i, sco.pop(i))

        def mul(i):
            last[0] = times_v(i, pts.pop(i), kvs[-1], at_free)

        def score(i):
            sco[i] = qk_scores(i, kq[i], kks[-1])
        for i in range(16):
            hooks = {0: [], 1: [], 2: []}
            if i == 0:
                hooks[0].append(lambda: vturn(*vt))
            if i >= 2:
                hooks[0].append(lambda i=i: turn(i - 2))
            if i >= 1:
                hooks[1].append(lambda i=i: score(i - 1))
            if i >= 2:
                hooks[2].append(lambda i=i: mul(i - 2))
            pi, bank, k = project(X, xk, hooks=hooks)
            kq[i], bf_ = rope(qr[i % 2][:, :], bank, k, st_["qr"][i % 2] or region_free[0])
            pa_free[pi] = bf_
        tail = {0: [lambda: turn(14), lambda: score(15)], 1: [lambda: mul(14)], 2: [lambda: turn(15), lambda: mul(15)]}
        return k, tail, last

    rcn = [0]
    rc_free = [k_x1A] * 2
    ev_free = [k_x1A] * 2

    stores = []

    def flush():
        while stores:
            stores.pop(0)()

    def wo_half(h, X, tail, last):
        for nb in range(16):
            s = rcn[0] % 2
            rcn[0] += 1
            kr_ = Q.D("sync", d_rc[s], rc[s][:, :], x1d[:, h, nb, :], rc_free[s], k_sx1, *kst.values())
            hk = {c: f + [flush] * (c == 0) for c, f in tail.items()} if nb == 0 else {0: [flush]}
            i, bank, k = project(X, [last[0]], hooks=hk, x3=last)
            k = V(lambda e, s=s, bank=bank: e.tensor_tensor(ev[s][:, :], bank[:, :], rc[s][:, :], ALU.add), k, kr_, ev_free[s])
            pa_free[i] = k
            rc_free[s] = k

            def store(s=s, nb=nb, k=k):
                ev_free[s] = Q.D("sync", d_o[s], x2d[:, h, nb, :], ev[s][:, :], k)
            stores.append(store)
        flush()
        return list(ev_free), k

    trib = cst[:, C_TRI:C_TRI + 64].rearrange("p (c j) -> p c j", j=8)

    def gate_steps(X, xk, need, out_):
        XHx, XLx = X
        g = Zg
        b1 = PT[1]
        while not xk:
            yield

        def fn(e, c):
            for kt in range(4 * c, 4 * c + 4):
                w = ggf[:, 16 * kt:16 * kt + 128]
                e.matmul(b1[:, :], w, XLx[:, kt, :], start=(kt == 0), stop=False)
                m = e.matmul(b1[:, :], w, XHx[:, kt, :], start=False, stop=(kt == 15))
            return m
        for c in range(4):
            k = T(lambda e, c=c: fn(e, c), xk[0], k_gw, st_["PT"][1])
            yield
        k = V(lambda e: e.tensor_copy(t2[0:16, :], b1[0:16, :]), k, need[0])
        yield

        def turn_g(e):
            for tb in range(4):
                m = e.transpose(b1[:, tb * 16:tb * 16 + 16], t2[0:16, tb * 128:tb * 128 + 128], ident[0:16, 0:16])
            return m
        k = T(turn_g, k)
        yield
        lg = g[:, 0:32]
        b3 = b1[:, 0:64].rearrange("p (a n) -> p a n", n=16)
        l3_ = lg.rearrange("p (a n) -> p a n", n=8)
        k = V(lambda e: e.tensor_copy(l3_, b3[:, :, 0:8]), k)
        k = V(lambda e: e.tensor_tensor(l3_, l3_, b3[:, :, 8:16], ALU.add), k)
        st_["PT"][1] = k
        G4 = g[:, 32:288].rearrange("p (a c j) -> p a c j", c=8, j=8)
        H4 = g[:, 288:544].rearrange("p (a c j) -> p a c j", c=8, j=8)
        for tb in range(4):
            lj = g[:, tb * 8:tb * 8 + 8].rearrange("p (a j) -> p a j", a=1).to_broadcast([128, 8, 8])
            lc = g[:, tb * 8:tb * 8 + 8].rearrange("p (c a) -> p c a", a=1).to_broadcast([128, 8, 8])
            k = V(lambda e, tb=tb, lj=lj, lc=lc: e.tensor_tensor(G4[:, tb, :, :], lj, lc, ALU.is_gt), k)
            k = V(lambda e, tb=tb, lj=lj, lc=lc: e.tensor_tensor(H4[:, tb, :, :], lj, lc, ALU.is_equal), k)
            k = V(lambda e, tb=tb: e.tensor_tensor(H4[:, tb, :, :], H4[:, tb, :, :], trib, ALU.mult), k)
        k = V(lambda e: e.tensor_tensor(g[:, 32:288], g[:, 32:288], g[:, 288:544], ALU.add), k)
        k = V(lambda e: e.tensor_reduce(g[:, 288:320], G4.rearrange("p a c j -> p (a c) j"), AX.X, ALU.add), k)
        k = V(lambda e: e.tensor_scalar(g[:, 288:320], g[:, 288:320], 2.0, None, ALU.is_lt), k)
        l3 = lg.rearrange("p (a c) -> p a c", c=8)
        k = V(lambda e: e.tensor_reduce(g[:, 320:324], l3, AX.X, ALU.max), k)
        k = V(lambda e: e.tensor_tensor(l3, l3, g[:, 320:324].rearrange("p (a c) -> p a c", c=1)
                                        .to_broadcast([128, 4, 8]), ALU.subtract), k)
        yield
        k = A(lambda e: e.activation(lg, lg, ACT.Exp), k)
        k = V(lambda e: e.tensor_tensor(lg, lg, g[:, 288:320], ALU.mult), k)
        k = V(lambda e: e.tensor_reduce(g[:, 320:324], l3, AX.X, ALU.add), k)
        k = V(lambda e: e.reciprocal(g[:, 324:328], g[:, 320:324]), k)
        k = V(lambda e: e.tensor_tensor(l3, l3, g[:, 324:328].rearrange("p (a c) -> p a c", c=1)
                                        .to_broadcast([128, 4, 8]), ALU.mult), k)
        yield
        b2 = PT[0]

        def fn2(e):
            for tb in range(4):
                m = e.transpose(b2[0:8, tb * 128:tb * 128 + 128], g[:, tb * 8:tb * 8 + 8], ident)
            return m
        kt_ = T(fn2, k, st_["PT"][0])
        yield
        kt_ = V(lambda e: e.tensor_copy(t2[0:8, :], b2[0:8, :]), kt_)
        yield
        kt_ = T(lambda e: e.matmul(b2[:, :], cst[0:8, C_SEL:C_SEL + 128], t2[0:8, :], start=True, stop=True), kt_)
        yield
        kt_ = V(lambda e: e.tensor_scalar(t2[:, :], b2[:, :], 2.0, None, ALU.mult), kt_)
        st_["PT"][0] = kt_
        out_[:] = [kt_]
        yield

    def ffn_half(h, X, xk, x2k, kg, low):
        i, bank, kp = project(X, [xk])
        kp = V(lambda e, bank=bank: e.tensor_tensor(t2[:, :], bank[:, :], t2[:, :], ALU.mult), kp, kg)
        pa_free[i] = kp
        a = A(lambda e: e.activation(low[0][:, :], t2[:, :], ACT.Copy), kp)
        kl_ = V(lambda e: e.tensor_tensor(low[1][:, :], t2[:, :], low[0][:, :].bitcast(F32), ALU.subtract), a)
        for nb in range(16):
            s = rcn[0] % 2
            rcn[0] += 1
            kr_ = Q.D("sync", d_rc[s], rc[s][:, :], x2d[:, h, nb, :], rc_free[s], *x2k)
            i, bank, k = project(X, [xk], (low[0], low[1], kl_), hooks={0: [flush]})
            k = V(lambda e, s=s, bank=bank, nb=nb: e.scalar_tensor_tensor(
                ev[s][:, :], bank[:, :], bbs[:, nb:nb + 1], rc[s][:, :], ALU.add, ALU.add), k, kr_, ev_free[s])
            pa_free[i] = k
            rc_free[s] = k

            def store(s=s, nb=nb, k=k):
                ev_free[s] = Q.D("sync", d_o[s], out[:, h, nb, :], ev[s][:, :], k)
            stores.append(store)
        flush()
        return k

    Zg = at(qr_off, [544])

    qkv_order = [16, 17, 18, 19, 20, 21, 22, 23] + list(range(16))
    for h in range(2):
        for nb in qkv_order:
            order(wblock(wqkv, nb))
        for nb in range(16):
            order(wblock(wo, nb))
    for h in range(2):
        order([(wl[:, 4 * c:4 * c + 4, :], 4) for c in range(4)])
        for nb in range(16):
            order(wblock(wb, nb, True))

    def finish():
        while steps:
            step()

    low = [(lgh, lgl), (at(mask_off, [HT], F32R), at(mask_off + 2 * KB, [HT], F32R))]
    XX = (XH_, XL_)
    AX2 = (ATH, ATL)
    r2, r3, g1, g2 = [], [], [], []
    feed()
    k_xrB = Q.D("sync", d_xr[1], AF0[:, :, :], xT[:, 1, :, :], k_sqd, gt_[HB - 1][1])
    steps.append(second_half(k_xrB))
    kxd, tail, last = qkv_attention((XL_, XH_), r1, k_x1B, k_sx1)
    r1 = []
    steps.append(later(4, ln_load(XF0[:, :, :], x1d[:, 1, :, :], [k_sx1, kxd])))
    steps.append(ln_steps(XF0, XF1, XH_, XL_, None, r1))
    ks2, kwo = wo_half(0, AX2, tail, last)
    finish()
    kxd2, tail, last = qkv_attention(XX, r1, [None], kwo)
    steps.append(later(4, ln_load(XF0[:, :, :], x2d[:, 0, :, :], [*ks2, kxd2])))
    steps.append(ln_steps(XF0, XF1, XH_, XL_, None, r2))
    steps.append(later(8, gate_steps(XX, r2, last, g1)))
    ks3, kwo2 = wo_half(1, AX2, tail, last)
    finish()
    steps.append(later(10, ln_load(AF1[:, :, :], x2d[:, 1, :, :], [*ks3, kwo2])))
    steps.append(ln_steps(AF1, AF0, ATH, ATL, None, r3))
    steps.append(later(8, gate_steps(AX2, r3, [kwo2], g2)))
    kf = ffn_half(0, XX, r2[0], ks2, g1[0], low[0])
    finish()
    ffn_half(1, AX2, r3[0], ks3, g2[0], low[1])
    Q.q["sync"].append((tuple(ev_free), None, None, 0))

    with nc.Block() as block:
        @block.sync
        def _(e):
            Q.emit("sync", e)

        @block.scalar
        def _(e):
            Q.emit("scalar", e)

        @block.gpsimd
        def _(e):
            Q.emit("gpsimd", e)

        @block.vector
        def _(e):
            Q.emit("vector", e)

        @block.tensor
        def _(e):
            Q.emit("tensor", e)
    return Q


def layout(x, ctx_4096, conv_w, gamma, beta, wq, wk, wv, wo, gate_w, base_w, base_b, lora_A, lora_B):
    f = lambda a: np.asarray(a)
    ac = np.ascontiguousarray
    x, ctx = f(x), f(ctx_4096)
    xt = ac(x.reshape(2, HT, 128, NT).transpose(2, 0, 3, 1))
    ctxT = ac(ctx.transpose(0, 2, 1))
    cols = np.array([(4 * (2 * j + s) + r) * 64 + d for j in range(4) for r in range(4) for s in range(2)
                     for d in range(64)])
    w = np.concatenate([f(wq)[:, cols], f(wk), f(wv)], axis=1)
    wqkv = ac(w.reshape(128, NT, 24, 128).transpose(2, 0, 1, 3))
    wo_ = ac(f(wo)[cols, :].reshape(16, 128, 128, NT).transpose(3, 1, 0, 2))
    la = f(lora_A).reshape(128, L).T
    wl = ac(la.reshape(128, NT, 128))
    bw = f(base_w).T.reshape(128, NT, 128, NT).transpose(3, 0, 1, 2)
    lb = f(lora_B).transpose(0, 2, 1).reshape(128, 128, NT).transpose(2, 0, 1)
    wb = ac(np.concatenate([bw, lb[:, :, None, :]], axis=2))
    gw = ac(f(gate_w).T.reshape(128, NT, 8))
    bb = ac(f(base_b).reshape(128, NT))
    cw = ac(np.broadcast_to(f(conv_w).reshape(1, 14), (128, 14)))
    bn = ac(np.broadcast_to(np.concatenate([f(gamma), f(beta)]).reshape(1, 2), (128, 2)))
    return dict(ctxT=ctxT, xT=xt, cw=cw, bn=bn, cst=constants(), rn=row_numbers(), wqkv=wqkv, wo=wo_, wl=wl, wb=wb, gw=gw, bb=bb)


def kernel(x, ctx_4096, L0_xattn_conv_w, L0_xattn_bn_gamma, L0_xattn_bn_beta, L0_attn_wq, L0_attn_wk, L0_attn_wv,
           L0_attn_wo, L0_ffn_gate_w, L0_ffn_base_w, L0_ffn_base_b, L0_ffn_lora_A, L0_ffn_lora_B):
    import concourse.bacc as bacc
    from concourse.bass_utils import run_bass_kernel_spmd

    arrays = layout(x, ctx_4096, L0_xattn_conv_w, L0_xattn_bn_gamma, L0_xattn_bn_beta, L0_attn_wq, L0_attn_wk,
                    L0_attn_wv, L0_attn_wo, L0_ffn_gate_w, L0_ffn_base_w, L0_ffn_base_b, L0_ffn_lora_A,
                    L0_ffn_lora_B)
    nc = bacc.Bacc("TRN2", target_bir_lowering=False, num_devices=1)
    args = [nc.dram_tensor(n, list(a.shape), F32, kind="ExternalInput").ap() for n, a in arrays.items()]
    out = nc.dram_tensor("out", [128, 2, NT, HT], F32, kind="ExternalOutput").ap()
    build(nc, *args, out)
    r = run_bass_kernel_spmd(nc, [arrays], core_ids=[0])
    got = r.results[0]["out"]
    return np.ascontiguousarray(got.transpose(1, 3, 0, 2)).reshape(B, C, L)
```
